# Optimizing a Trainium2 kernel written in Bass

```python
import numpy as np
import jax
import jax.numpy as jnp

def _softmax(x, axis=-1):
    return jax.nn.softmax(x, axis=axis)

def _gelu(x):
    return jax.nn.gelu(x, approximate=True)

def _silu(x):
    return jax.nn.silu(x)

def _sigmoid(x):
    return jax.nn.sigmoid(x)

def _layernorm(x, axis=-1, eps=1e-05):
    m = jnp.mean(x, axis=axis, keepdims=True)
    v = jnp.var(x, axis=axis, keepdims=True)
    return (x - m) / jnp.sqrt(v + eps)

def _scatter_add(tgt, idx, src, axis=0):
    return tgt.at[idx].add(src)

def _segment_sum(src, seg, n):
    return jax.ops.segment_sum(src, seg, n)
kernel_name = 'mk_prb_d1_jaxref_r8_e23d6b'

def setup_inputs(seed: int=0):
    np.random.seed(seed)
    _w = jnp.asarray

    def _L0_attn_setup():
        import jax, jax.numpy as jnp
        import numpy as np
        HIDDEN = 128
        HEADS = 16
        HEAD = HIDDEN // HEADS

        def _ternary_weight(key, shape):
            g = jax.random.normal(key, shape, dtype=jnp.float32)
            return jnp.where(jnp.abs(g) < 0.6, 0.0, jnp.sign(g)).astype(jnp.float32)

        def _tlin(x, w, s, b):
            return jnp.einsum('bsh,oh->bso', x, w) * s + b
        key = jax.random.key(seed)
        ks = jax.random.split(key, 10)
        x = jax.random.normal(ks[0], (2, 256, HIDDEN), dtype=jnp.float32)
        d = {'x': x}
        names = ['q', 'k', 'v', 'o']
        for i, n in enumerate(names):
            d[f'w_{n}'] = _ternary_weight(ks[1 + i], (HIDDEN, HIDDEN))
            d[f's_{n}'] = jnp.float32(0.02)
            d[f'b_{n}'] = jax.random.normal(ks[5 + i], (HIDDEN,), dtype=jnp.float32) * 0.02
        return d
    _L0_attn_in = _L0_attn_setup()

    def _L0_ffn_setup():
        import jax, jax.numpy as jnp
        import numpy as np
        import math
        D_IN = 128
        FEATURES = (512, 512, 128)
        BATCH, SEQ = (8, 256)

        def _conn_dense(kernel_bool, x):
            w = jnp.where(kernel_bool, jnp.float32(1.0), jnp.float32(-1.0))
            return x @ w
        key = jax.random.key(seed)
        kx, kk0, kk1, kk2 = jax.random.split(key, 4)
        x = jax.random.normal(kx, (BATCH, SEQ, D_IN), dtype=jnp.float32)
        k0 = jax.random.randint(kk0, (2 * D_IN, FEATURES[0]), 0, 2).astype(jnp.bool_)
        k1 = jax.random.randint(kk1, (FEATURES[0], FEATURES[1]), 0, 2).astype(jnp.bool_)
        k2 = jax.random.randint(kk2, (FEATURES[1], FEATURES[2]), 0, 2).astype(jnp.bool_)
        s0 = jnp.asarray(1.0 / math.sqrt(2 * D_IN), dtype=jnp.float32)
        s1 = jnp.asarray(1.0 / math.sqrt(FEATURES[0]), dtype=jnp.float32)
        s2 = jnp.asarray(1.0 / math.sqrt(FEATURES[1]), dtype=jnp.float32)
        return {'x': x, 'k0': k0, 'k1': k1, 'k2': k2, 's0': s0, 's1': s1, 's2': s2}
    _L0_ffn_in = _L0_ffn_setup()
    _d = {'L0_attn_x': _L0_attn_in['x'], 'L0_attn_w_q': _L0_attn_in['w_q'], 'L0_attn_s_q': _L0_attn_in['s_q'], 'L0_attn_b_q': _L0_attn_in['b_q'], 'L0_attn_w_k': _L0_attn_in['w_k'], 'L0_attn_s_k': _L0_attn_in['s_k'], 'L0_attn_b_k': _L0_attn_in['b_k'], 'L0_attn_w_v': _L0_attn_in['w_v'], 'L0_attn_s_v': _L0_attn_in['s_v'], 'L0_attn_b_v': _L0_attn_in['b_v'], 'L0_attn_w_o': _L0_attn_in['w_o'], 'L0_attn_s_o': _L0_attn_in['s_o'], 'L0_attn_b_o': _L0_attn_in['b_o'], 'L0_ffn_k0': _L0_ffn_in['k0'], 'L0_ffn_k1': _L0_ffn_in['k1'], 'L0_ffn_k2': _L0_ffn_in['k2'], 'L0_ffn_s0': _L0_ffn_in['s0'], 'L0_ffn_s1': _L0_ffn_in['s1'], 'L0_ffn_s2': _L0_ffn_in['s2']}
    _x0 = _d['L0_attn_x']
    _d['L0_attn_x'] = jax.random.normal(jax.random.fold_in(jax.random.key(seed), 1), (16, 256, 128), dtype=_x0.dtype)
    del _x0
    return _d

def reference(L0_attn_x, L0_attn_w_q, L0_attn_s_q, L0_attn_b_q, L0_attn_w_k, L0_attn_s_k, L0_attn_b_k, L0_attn_w_v, L0_attn_s_v, L0_attn_b_v, L0_attn_w_o, L0_attn_s_o, L0_attn_b_o, L0_ffn_k0, L0_ffn_k1, L0_ffn_k2, L0_ffn_s0, L0_ffn_s1, L0_ffn_s2):

    def _L0_attn_ref(x, w_q, s_q, b_q, w_k, s_k, b_k, w_v, s_v, b_v, w_o, s_o, b_o):
        import jax, jax.numpy as jnp
        import numpy as np
        HIDDEN = 128
        HEADS = 16
        HEAD = HIDDEN // HEADS

        def _ternary_weight(key, shape):
            g = jax.random.normal(key, shape, dtype=jnp.float32)
            return jnp.where(jnp.abs(g) < 0.6, 0.0, jnp.sign(g)).astype(jnp.float32)

        def _tlin(x, w, s, b):
            return jnp.einsum('bsh,oh->bso', x, w) * s + b
        B, S, H = x.shape

        def split_heads(t):
            return t.reshape(B, S, HEADS, HEAD).transpose(0, 2, 1, 3)
        q = split_heads(_tlin(x, w_q, s_q, b_q))
        k = split_heads(_tlin(x, w_k, s_k, b_k))
        v = split_heads(_tlin(x, w_v, s_v, b_v))
        scores = jnp.einsum('bhqd,bhkd->bhqk', q, k) / jnp.sqrt(jnp.float32(HEAD))
        attn = jax.nn.softmax(scores, axis=-1)
        ctx = jnp.einsum('bhqk,bhkd->bhqd', attn, v)
        ctx = ctx.transpose(0, 2, 1, 3).reshape(B, S, H)
        return _tlin(ctx, w_o, s_o, b_o)

    def _L0_ffn_ref(x, k0, k1, k2, s0, s1, s2):
        import jax, jax.numpy as jnp
        import numpy as np
        import math
        D_IN = 128
        FEATURES = (512, 512, 128)
        BATCH, SEQ = (8, 256)

        def _conn_dense(kernel_bool, x):
            w = jnp.where(kernel_bool, jnp.float32(1.0), jnp.float32(-1.0))
            return x @ w
        h = jnp.concatenate([x, -x], axis=-1)
        h = s0 * _conn_dense(k0, h)
        h = jax.nn.relu(h) * 2
        h = s1 * _conn_dense(k1, h)
        h = jax.nn.relu(h) * 2
        h = s2 * _conn_dense(k2, h)
        return h
    x = L0_attn_x
    xn = _layernorm(x, axis=-1)
    x = x + _L0_attn_ref(xn, L0_attn_w_q, L0_attn_s_q, L0_attn_b_q, L0_attn_w_k, L0_attn_s_k, L0_attn_b_k, L0_attn_w_v, L0_attn_s_v, L0_attn_b_v, L0_attn_w_o, L0_attn_s_o, L0_attn_b_o) + _L0_ffn_ref(xn, L0_ffn_k0, L0_ffn_k1, L0_ffn_k2, L0_ffn_s0, L0_ffn_s1, L0_ffn_s2)
    return x

_drawn_inputs = setup_inputs


def setup_inputs(seed=0):
    import zlib

    import numpy as np

    out = dict(_drawn_inputs(seed))
    spreads = {}
    factors = {'L0_attn_w_q': 8.0,
     'L0_attn_b_q': 8.0,
     'L0_attn_w_k': 8.0,
     'L0_attn_b_k': 8.0,
     'L0_attn_w_v': 8.0,
     'L0_attn_b_v': 8.0,
     'L0_attn_w_o': 8.0,
     'L0_attn_b_o': 5.915}
    for name, (base, spread) in spreads.items():
        noise = np.random.default_rng([zlib.crc32(name.encode()), seed]).standard_normal(out[name].shape)
        drawn = base * np.exp(spread * noise) if base else spread * noise
        out[name] = jnp.asarray(drawn.astype(out[name].dtype))
    for name, factor in factors.items():
        out[name] = (out[name] * factor).astype(out[name].dtype)
    return out
```

```python
from contextlib import ExitStack

import concourse.bass as bass
from concourse import mybir

BATCH, SEQ, HID = 16, 256, 128
HEADS, DH = 16, 8
HALF = HEADS // 2
FEAT = 512
P = 128
TT = SEQ // P
FB = FEAT // P
PARTS = 3
ROWS = DH * PARTS * PARTS
MROWS = ROWS + PARTS
GROUP = 4
GROUPS = HEADS // GROUP
VC = 32
EPS = 1e-5
EXP_SCALE = float(DH) ** -0.5
X_UP = 2.0 ** 12
W0_DOWN = 2.0 ** -4
W1_DOWN = 2.0 ** -9
FFN_SCALE = 2.0 * 2.0 * 2.0 / (X_UP * W0_DOWN * W1_DOWN)
LOOP_FIRST, LOOP_STEPS = 3, 12
LAST_STEP = BATCH + 2


class Step:

    def __init__(self, first, loop=None):
        self.first, self.loop = first, loop

    def count(self, per_step, const):
        if self.loop is None:
            return per_step * self.first + const
        return self.loop * (2 * per_step) + (per_step * self.first + const)

    def has(self, lag):
        return self.loop is not None or 0 <= self.first - lag < BATCH

    def batch(self, lag):
        return self.count(1, -lag)

    def par(self, lag):
        return (self.first - lag) % 2

    def wait(self, eng, sem, per_batch, lag, k):
        v = self.count(per_batch, k - per_batch * lag)
        if self.loop is not None or v > 0:
            eng.wait_ge(sem, v)

    def wait_dma(self, eng, sems, lag, later=1):
        q = self.par(lag)
        v = self.count(8, -8 * lag - 8 * q + 16 * later)
        if self.loop is not None or v > 0:
            eng.wait_ge(sems[q], v)


def run_steps(eng, step):
    for i in range(-1, LOOP_FIRST):
        step(Step(i))
    with eng.Fori(0, LOOP_STEPS // 2) as it:
        step(Step(LOOP_FIRST, it))
        step(Step(LOOP_FIRST + 1, it))
    for i in range(LOOP_FIRST + LOOP_STEPS, LAST_STEP + 1):
        step(Step(i))


def build(nc, x, w4, bqk, bvo, sc7, k0, k1, k2, out):
    f32, bf16, f16, u8 = mybir.dt.float32, mybir.dt.bfloat16, mybir.dt.float16, mybir.dt.uint8
    ALU, ACT, AX = mybir.AluOpType, mybir.ActivationFunctionType, mybir.AxisListType

    scratch = nc.dram_tensor("qk_scratch", (2, 2 * DH, PARTS, HALF, SEQ), bf16, kind="Internal").ap()

    with ExitStack() as ctx:
        def sb(name, shape, dt):
            return ctx.enter_context(nc.sbuf_tensor(name, shape, dt))

        def sem(name):
            return ctx.enter_context(nc.semaphore(name))

        w_sb = sb("w_sb", [P, 4, HID], f32)
        bqk_sb = sb("bqk_sb", [P, 2], f32)
        bvo_sb = sb("bvo_sb", [P, 2, HID], f32)
        sc_sb = sb("sc_sb", [P, 7], f32)
        k0_sb = sb("k0_sb", [P, 2, FEAT], u8)
        k1_sb = sb("k1_sb", [P, FB, FEAT], u8)
        k2_sb = sb("k2_sb", [P, FB, HID], u8)
        w0d = sb("w0d", [P, FEAT], f16)
        w0 = sb("w0", [P, FEAT], f16)
        w1 = sb("w1", [P, FB, FEAT], f16)
        w2 = sb("w2", [P, FB, HID], f16)
        sgn = sb("sgn", [P, 8], f32)
        ffn_scale = sb("ffn_scale", [P, 1], f32)
        ident = sb("ident", [P, P], f32)
        ident16 = sb("ident16", [P, P], bf16)
        xin = [sb(f"xin{n}", [P, TT, HID], f32) for n in range(2)]
        stats = sb("stats", [P, TT, 6], f32)
        meanvar = sb("meanvar", [P, TT, 2], f32)
        var_eps = sb("var_eps", [P, TT], f32)
        minus_half = sb("minus_half", [P, TT], f32)
        rstd = sb("rstd", [P, TT], f32)
        xn = sb("xn", [P, TT, HID], f32)
        xres = [sb(f"xres{n}", [P, TT, HID], f32) for n in range(2)]
        xT = [sb(f"xT{n}", [P, SEQ], f32) for n in range(2)]
        xT_hi = [sb(f"xT_hi{n}", [P, SEQ], f16) for n in range(2)]
        xT_lo = [sb(f"xT_lo{n}", [P, SEQ], f16) for n in range(2)]
        qk = sb("qk", [P, 2, SEQ], f32)
        qk_rest = sb("qk_rest", [P, 2, SEQ], f32)
        qk_part = sb("qk_part", [P, PARTS, 2, SEQ], bf16)
        q_rows = [sb(f"q_rows{n}", [P, HEADS * SEQ], bf16) for n in range(2)]
        k_rows = [sb(f"k_rows{n}", [P, HEADS * SEQ], bf16) for n in range(2)]
        neg_max = sb("neg_max", [P, 2, HALF, TT], f32)
        max_rest = sb("max_rest", [P, 2, HALF * TT], f32)
        max_part = sb("max_part", [P, 2, P], bf16)
        max_rows = [sb(f"max_rows{n}", [PARTS * HALF * TT, P], bf16) for n in range(2)]
        v_ext = [sb(f"v_ext{n}", [P, TT, HEADS, VC], f32) for n in range(2)]
        r0_hi = sb("r0_hi", [P, FB, SEQ], f16)
        r0_lo = sb("r0_lo", [P, FB, SEQ], f16)
        r1_hi = sb("r1_hi", [P, FB, SEQ], f16)
        r1_lo = sb("r1_lo", [P, FB, SEQ], f16)
        y = [sb(f"y{n}", [P, TT, HID], f32) for n in range(2)]
        probs = [sb(f"probs{n}", [P, GROUP, TT, SEQ], f32) for n in range(2)]
        ctx_sb = sb("ctx_sb", [P, GROUPS, SEQ], f32)
        rden = sb("rden", [P, TT, HEADS], f32)
        ctxn = sb("ctxn", [P, TT, HID], f32)
        ctxT = sb("ctxT", [P, SEQ], f32)
        outs = [sb(f"outs{n}", [P, TT, HID], f32) for n in range(2)]

        def bank(name):
            return ctx.enter_context(nc.psum_tensor(name, [P, 2 * SEQ], f32))

        s_bank = [bank(f"s_bank{n}") for n in range(2)]
        st_bank = [bank(f"st_bank{n}") for n in range(2)]
        ctx_bank = bank("ctx_bank")
        work = [bank(f"work{n}") for n in range(2)]

        weights_loaded = sem("weights_loaded")
        x_loaded = [sem(f"x_loaded{n}") for n in range(2)]
        parts_stored = sem("parts_stored")
        rows_loaded = [sem(f"rows_loaded{n}") for n in range(2)]
        max_rows_loaded = [sem(f"max_rows_loaded{n}") for n in range(2)]
        out_stored = [sem(f"out_stored{n}") for n in range(2)]
        ident_zeroed = sem("ident_zeroed")
        ident_ready = sem("ident_ready")
        ones_ready = sem("ones_ready")
        v_zeroed = sem("v_zeroed")
        v_ones_ready = sem("v_ones_ready")
        setup_step = sem("setup_step")
        ffn_weights_ready = sem("ffn_weights_ready")
        ln_step = sem("ln_step")
        half_ready = sem("half_ready")
        var_eps_ready = sem("var_eps_ready")
        rstd_ready = sem("rstd_ready")
        xn_ready = sem("xn_ready")
        xres_ready = sem("xres_ready")
        xT_psum = sem("xT_psum")
        xT_copied = sem("xT_copied")
        xT_split = sem("xT_split")
        qk_psum = sem("qk_psum")
        qk_scaled = sem("qk_scaled")
        qk_hi_ready = sem("qk_hi_ready")
        qk_rest_ready = sem("qk_rest_ready")
        qk_mid_ready = sem("qk_mid_ready")
        parts_ready = sem("parts_ready")
        s_psum = sem("s_psum")
        max_ready = sem("max_ready")
        max_split_step = sem("max_split_step")
        max_part_zeroed = sem("max_part_zeroed")
        max_parts_ready = sem("max_parts_ready")
        maxT_psum = sem("maxT_psum")
        max_rows_ready = sem("max_rows_ready")
        v_psum = sem("v_psum")
        v_ready = sem("v_ready")
        l0_psum = sem("l0_psum")
        r0_hi_ready = sem("r0_hi_ready")
        r0_ready = sem("r0_ready")
        l1_psum = sem("l1_psum")
        r1_hi_ready = sem("r1_hi_ready")
        r1_ready = sem("r1_ready")
        l2_psum = sem("l2_psum")
        y_ready = sem("y_ready")
        st_psum = sem("st_psum")
        probs_ready = sem("probs_ready")
        ctx_psum = sem("ctx_psum")
        ctx_copied = sem("ctx_copied")
        ctx_turned = sem("ctx_turned")
        rden_ready = sem("rden_ready")
        ctxn_ready = sem("ctxn_ready")
        ctxT_psum = sem("ctxT_psum")
        ctxT_ready = sem("ctxT_ready")
        o_psum = sem("o_psum")
        out_ready = sem("out_ready")

        N_WEIGHT_DMAS = 7
        LOADS = 16 * 2 * PARTS
        STORES = 16 * 2 * PARTS
        block = ctx.enter_context(nc.Block())

        @block.sync
        def _(sp):
            def step(s):
                load_batch = sp.snap(s.batch(-1)) if s.loop is not None else s.batch(-1)
                store_batch = sp.snap(s.batch(3)) if s.loop is not None else s.batch(3)
                rows_free = [s.count(HEADS, HALF * (h + 1) - 2 * HEADS) for h in range(2)]
                if s.loop is not None:
                    rows_free = [sp.snap(sp.to_reg(v)) for v in rows_free]
                if s.has(2):
                    s.wait(sp, max_rows_ready, 2, 2, 2)
                    sp.dma_start(q_rows[s.par(2)][ROWS:MROWS, HALF * SEQ:], max_rows[1][:, :]
                                 ).then_inc(max_rows_loaded[1], 16)
                if s.has(-1):
                    s.wait(sp, xn_ready, 1, 1, 1)
                    s.wait(sp, xres_ready, 1, 1, 1)
                    sp.dma_start(xin[s.par(-1)][:, :, :],
                                 x[bass.ds(load_batch, 1), :, :].rearrange("a (t p) c -> p (a t) c", p=P)
                                 ).then_inc(x_loaded[s.par(-1)], 16)
                if s.first == -1:
                    load_weights()
                if s.has(0):
                    s.wait(sp, parts_ready, 1, 0, 1)
                    for h in range(2):
                        s.wait(sp, rows_loaded[h], LOADS, 1, LOADS)
                    for n in range(2):
                        for r in range(PARTS):
                            sp.dma_start(scratch[n, :, r], qk_part[:, r, n, :]).then_inc(parts_stored, 16)
                if s.has(3):
                    s.wait(sp, out_ready, 1, 3, 1)
                    sp.dma_start(out[bass.ds(store_batch, 1), :, :].rearrange("a (t p) c -> p (a t) c", p=P),
                                 outs[s.par(3)][:, :, :]).then_inc(out_stored[s.par(3)], 16)
                for h in range(2):
                    if h == 1 and s.has(1):
                        s.wait(sp, max_rows_ready, 2, 1, 1)
                        sp.dma_start(q_rows[s.par(1)][ROWS:MROWS, :HALF * SEQ], max_rows[0][:, :]
                                     ).then_inc(max_rows_loaded[0], 16)
                    if s.has(0):
                        if h == 0:
                            s.wait(sp, parts_stored, STORES, 0, STORES)
                        if s.has(2):
                            sp.wait_ge(st_psum, rows_free[h])
                        if s.first == 0 and h == 0:
                            sp.wait_ge(ones_ready, 2)
                        q_src = scratch[0, DH * h:DH * (h + 1)].rearrange("d r h t -> d r (h t)")
                        k_src = scratch[1, DH * h:DH * (h + 1)].rearrange("d r h t -> (d r) (h t)")
                        cols = slice(h * HALF * SEQ, (h + 1) * HALF * SEQ)
                        for a in range(PARTS):
                            rows = slice(a * DH * PARTS, (a + 1) * DH * PARTS)
                            sp.dma_start(q_rows[s.par(0)][rows, cols],
                                         q_src[:, a:a + 1, :].to_broadcast([DH, PARTS, HALF * SEQ])
                                         ).then_inc(rows_loaded[h], 16)
                            sp.dma_start(k_rows[s.par(0)][rows, cols], k_src).then_inc(rows_loaded[h], 16)

            def load_weights():
                for dst, src in ((w_sb[:, :, :], w4), (bqk_sb[:, :], bqk),
                                 (sc_sb[:, :], sc7.to_broadcast([P, 7])),
                                 (bvo_sb[:, :, :].rearrange("p a c -> p (a c)"), bvo.to_broadcast([P, 2 * HID])),
                                 (k0_sb[:, :, :].bitcast(mybir.dt.uint32), k0.rearrange("(a p) f -> p a f", p=P)),
                                 (k1_sb[:, :, :].bitcast(mybir.dt.uint32), k1.rearrange("(a p) f -> p a f", p=P)),
                                 (k2_sb[:, :, :].bitcast(mybir.dt.uint32), k2.rearrange("(a p) f -> p a f", p=P))):
                    sp.dma_start(dst, src).then_inc(weights_loaded, 16)

            run_steps(sp, step)
            for n in range(2):
                sp.wait_ge(out_stored[n], 16 * BATCH // 2)

        @block.gpsimd
        def _(pool):
            def step(s):
                if s.has(0):
                    residual_and_parts(s)
                if s.has(-1):
                    s.wait(pool, var_eps_ready, 1, -1, 1)
                    nc.gpsimd.tensor_tensor(rstd[:, :], var_eps[:, :], minus_half[:, :], ALU.pow
                                            ).then_inc(rstd_ready, 1)

                if s.first == 0:
                    for n in range(2):
                        nc.gpsimd.memset(v_ext[n][:, :, :, :], 0.0).then_inc(v_zeroed, 1)
                    pool.wait_ge(v_zeroed, 2)
                    for n in range(2):
                        nc.gpsimd.memset(v_ext[n][:, :, :, DH:DH + 1], 1.0).then_inc(v_ones_ready, 1)

            def residual_and_parts(s):
                if s.first == 0:
                    pool.wait_ge(weights_loaded, 16 * N_WEIGHT_DMAS)
                s.wait_dma(pool, x_loaded, 0)
                s.wait(pool, y_ready, 1, 2, 1)
                nc.gpsimd.tensor_tensor(xres[s.par(0)][:, :, :], xin[s.par(0)][:, :, :],
                                        bvo_sb[:, 1:2, :].to_broadcast([P, TT, HID]), ALU.add
                                        ).then_inc(xres_ready, 1)
                s.wait(pool, qk_hi_ready, 1, 0, 1)
                nc.gpsimd.tensor_tensor(qk_rest[:, :, :], qk[:, :, :], qk_part[:, 0], ALU.subtract
                                        ).then_inc(qk_rest_ready, 1)
                s.wait(pool, qk_mid_ready, 1, 0, 1)
                nc.gpsimd.tensor_tensor(qk_part[:, 2], qk_rest[:, :, :], qk_part[:, 1], ALU.subtract
                                        ).then_inc(parts_ready, 1)

            nc.gpsimd.memset(minus_half[:, :], -0.5).then_inc(half_ready, 1)
            pool.wait_ge(half_ready, 1)
            nc.gpsimd.memset(ident[:, :], 0.0).then_inc(ident_zeroed, 1)
            nc.gpsimd.memset(ident16[:, :], 0.0).then_inc(ident_zeroed, 1)
            pool.wait_ge(ident_zeroed, 2)
            for m in (ident, ident16):
                nc.gpsimd.affine_select(out=m[:, :], in_=m[:, :], compare_op=ALU.not_equal, fill=1.0, base=0,
                                        pattern=[[-1, P]], channel_multiplier=1).then_inc(ident_ready, 1)
            run_steps(pool, step)

        @block.scalar
        def _(act):
            def context_copy(s, lag, g):
                s.wait(act, ctx_psum, GROUPS, lag, g + 1)
                if g == 0:
                    s.wait(act, ctx_turned, TT, lag + 1, TT)
                nc.scalar.activation(ctx_sb[:, g, :], ctx_bank[:, 0:SEQ], ACT.Copy).then_inc(ctx_copied, 1)

            def relu_hi(s, k, psum, dst, ready, b):
                nc.scalar.activation(dst[:, 2 * k:2 * k + 2, :].rearrange("p m t -> p (m t)"), b[:, :],
                                     ACT.Relu).then_inc(ready, 1)

            def step(s):
                for t in range(HEADS):
                    if s.has(2):
                        s.wait(act, st_psum, HEADS, 2, t + 1)
                        if t % GROUP == 0:
                            s.wait(act, ctx_psum, GROUPS, 2, t // GROUP - 1)
                        nc.scalar.activation(
                            probs[t // GROUP % 2][:, t % GROUP, :, :].rearrange("p k q -> p (k q)"),
                            st_bank[t % 2][:, :], ACT.Exp, scale=EXP_SCALE).then_inc(probs_ready, 1)
                    if t == 1 and s.has(1):
                        s.wait(act, l0_psum, 2, 1, 1)
                        s.wait(act, l1_psum, 2, 2, 2)
                        relu_hi(s, 0, l0_psum, r0_hi, r0_hi_ready, work[0])
                    if t == 1 and s.has(0):
                        s.wait(act, xT_psum, 1, 0, 1)
                        s.wait(act, v_psum, 1, 2, 1)
                        s.wait(act, l0_psum, 2, 2, 2)
                        nc.scalar.activation(xT[s.par(0)][:, :], work[1][:, 0:SEQ], ACT.Copy).then_inc(xT_copied, 1)
                        nc.scalar.activation(xT_hi[s.par(0)][:, :], work[1][:, 0:SEQ], ACT.Copy, scale=X_UP
                                             ).then_inc(xT_copied, 1)
                    if t == 2 and s.has(3):
                        context_copy(s, 3, GROUPS - 1)
                    if t == 3 and s.has(0):
                        s.wait(act, qk_psum, 1, 0, 1)
                        s.wait(act, parts_ready, 1, 1, 1)
                        s.wait(act, parts_stored, STORES, 1, STORES)
                        for n in range(2):
                            nc.scalar.activation(qk[:, n, :], work[0][:, n * SEQ:(n + 1) * SEQ], ACT.Identity,
                                                 scale=sc_sb[:, n:n + 1], bias=bqk_sb[:, n:n + 1]
                                                 ).then_inc(qk_scaled, 1)
                        s.wait(act, qk_scaled, 2, 0, 2)
                        nc.scalar.activation(qk_part[:, 0], qk[:, :, :], ACT.Copy).then_inc(qk_hi_ready, 1)
                    if t == 4 and s.has(1):
                        s.wait(act, l0_psum, 2, 1, 2)
                        relu_hi(s, 1, l0_psum, r0_hi, r0_hi_ready, work[1])
                    if t == 5 and s.has(0):
                        s.wait(act, qk_rest_ready, 1, 0, 1)
                        nc.scalar.activation(qk_part[:, 1], qk_rest[:, :, :], ACT.Copy).then_inc(qk_mid_ready, 1)
                    if t == 6 and s.has(2):
                        context_copy(s, 2, 0)
                    if t == 7 and s.has(3):
                        s.wait(act, ctxT_psum, 1, 3, 1)
                        s.wait(act, o_psum, 1, 4, 1)
                        nc.scalar.activation(ctxT[:, :], work[1][:, 0:SEQ], ACT.Copy).then_inc(ctxT_ready, 1)
                    if t == 10 and s.has(2):
                        context_copy(s, 2, 1)
                    if t == 11 and s.has(1):
                        s.wait(act, l1_psum, 2, 1, 1)
                        s.wait(act, l2_psum, 1, 2, 1)
                        relu_hi(s, 0, l1_psum, r1_hi, r1_hi_ready, work[0])
                    if t == 13 and s.has(1):
                        s.wait(act, l1_psum, 2, 1, 2)
                        relu_hi(s, 1, l1_psum, r1_hi, r1_hi_ready, work[1])
                    if t == 14 and s.has(2):
                        context_copy(s, 2, 2)

            act.wait_ge(weights_loaded, 16 * N_WEIGHT_DMAS)
            run_steps(act, step)

        @block.vector
        def _(dve):
            def token_stats(s):
                s.wait_dma(dve, x_loaded, -1)
                for t in range(TT):
                    nc.vector.bn_stats(stats[:, t, :], xin[s.par(-1)][:, t, :]).then_inc(ln_step, 1)

            def layer_norm(s):
                xb = xin[s.par(-1)]
                for t in range(TT):
                    nc.vector.bn_aggr(meanvar[:, t, :], stats[:, t, :]).then_inc(ln_step, 1)
                s.wait(dve, ln_step, 2 * TT, -1, 2 * TT)
                nc.vector.tensor_scalar(var_eps[:, :], meanvar[:, :, 1], EPS, None, ALU.add
                                        ).then_inc(var_eps_ready, 1)
                s.wait(dve, rstd_ready, 1, -1, 1)
                s.wait(dve, xT_psum, 1, 0, 1)
                for t in range(TT):
                    last = nc.vector.tensor_scalar(xn[:, t, :], xb[:, t, :], meanvar[:, t, 0:1],
                                                   rstd[:, t:t + 1], ALU.subtract, ALU.mult)
                last.then_inc(xn_ready, 1)

            def split_max(s, half):
                full = neg_max[:, half, :, :].rearrange("p h t -> p (h t)")
                rest = max_rest[:, half, :]
                part = max_part[:, half, 0:PARTS * HALF * TT].rearrange("p (r c) -> p r c", r=PARTS)
                s.wait(dve, max_ready, HEADS, 1, HALF * (half + 1))
                s.wait(dve, maxT_psum, 2, 2, half + 1)
                nc.vector.tensor_copy(part[:, 0, :], full).then_inc(max_split_step, 1)
                s.wait(dve, max_split_step, 6, 1, 3 * half + 1)
                nc.vector.tensor_tensor(rest, full, part[:, 0, :], ALU.subtract).then_inc(max_split_step, 1)
                s.wait(dve, max_split_step, 6, 1, 3 * half + 2)
                nc.vector.tensor_copy(part[:, 1, :], rest).then_inc(max_split_step, 1)
                s.wait(dve, max_split_step, 6, 1, 3 * half + 3)
                nc.vector.tensor_tensor(part[:, 2, :], rest, part[:, 1, :], ALU.subtract
                                        ).then_inc(max_parts_ready, 1)

            def copy_max_rows(s, lag, half):
                s.wait(dve, maxT_psum, 2, lag, half + 1)
                s.wait(dve, max_rows_loaded[half], 16, lag + 1, 16)
                src = work[0][:, :].bitcast(bf16)
                nc.vector.tensor_copy(max_rows[half][:, :], src[0:PARTS * HALF * TT, 0:P]
                                      ).then_inc(max_rows_ready, 1)

            def relu_lo(k, b, hi, lo, ready):
                nc.vector.scalar_tensor_tensor(
                    out=lo[:, 2 * k:2 * k + 2, :].rearrange("p m t -> p (m t)"), in0=b[:, :], scalar=0.0,
                    in1=hi[:, 2 * k:2 * k + 2, :].rearrange("p m t -> p (m t)"),
                    op0=ALU.max, op1=ALU.subtract).then_inc(ready, 1)

            def step(s):
                if s.first == 0:
                    for n in range(2):
                        nc.vector.memset(k_rows[n][64:MROWS, :], 1.0).then_inc(ones_ready, 1)
                    ffn_weights()
                for t in range(HEADS):
                    if t == 10 and s.has(-1):
                        s.wait(dve, ln_step, 2 * TT, -1, TT)
                    if s.has(1):
                        s.wait(dve, s_psum, HEADS, 1, t + 1)
                        nc.vector.tensor_reduce(out=neg_max[:, t // HALF, t % HALF, :],
                                                in_=s_bank[t % 2][:, :].rearrange("p (q k) -> p q k", q=TT),
                                                op=ALU.max, axis=AX.X, negate=True).then_inc(max_ready, 1)
                    if t == 0 and s.has(2):
                        s.wait(dve, l2_psum, 1, 2, 1)
                        s.wait(dve, xres_ready, 1, 2, 1)
                        nc.vector.scalar_tensor_tensor(
                            out=y[s.par(2)][:, :, :].rearrange("p t c -> p (t c)"), in0=work[1][:, 0:TT * HID],
                            scalar=ffn_scale[:, :], in1=xres[s.par(2)][:, :, :].rearrange("p t c -> p (t c)"),
                            op0=ALU.mult, op1=ALU.add).then_inc(y_ready, 1)
                    if t == 1 and s.has(1):
                        s.wait(dve, r0_hi_ready, 2, 1, 1)
                        s.wait(dve, l1_psum, 2, 2, 2)
                        relu_lo(0, work[0], r0_hi, r0_lo, r0_ready)
                    if t == 1 and s.has(0):
                        s.wait(dve, xT_copied, 2, 0, 2)
                        s.wait(dve, l0_psum, 2, 2, 2)
                        nc.vector.scalar_tensor_tensor(
                            out=xT_lo[s.par(0)][:, :], in0=work[1][:, 0:SEQ], scalar=X_UP,
                            in1=xT_hi[s.par(0)][:, :], op0=ALU.mult, op1=ALU.subtract).then_inc(xT_split, 1)
                    if t == 4 and s.has(1):
                        s.wait(dve, r0_hi_ready, 2, 1, 2)
                        relu_lo(1, work[1], r0_hi, r0_lo, r0_ready)
                    if t == 4 and s.has(2):
                        copy_max_rows(s, 2, 1)
                    if t == 5 and s.has(3):
                        for q in range(TT):
                            s.wait(dve, ctx_turned, TT, 3, q + 1)
                            s.wait(dve, ctxT_psum, 1, 4, 1)
                            heads = work[(q + 1) % 2][:, :].rearrange("p (h c) -> p h c", c=VC)
                            nc.vector.reciprocal(rden[:, q, :], heads[:, :, DH]).then_inc(rden_ready, 1)
                            s.wait(dve, rden_ready, TT, 3, q + 1)
                            nc.vector.tensor_tensor(
                                ctxn[:, q, :].rearrange("p (h d) -> p h d", d=DH), heads[:, :, 0:DH],
                                rden[:, q, :].unsqueeze(2).to_broadcast([P, HEADS, DH]), ALU.mult
                            ).then_inc(ctxn_ready, 1)
                    if t == 7 and s.has(1):
                        s.wait(dve, v_psum, 1, 1, 1)
                        s.wait(dve, ctx_psum, GROUPS, 3, GROUPS)
                        if s.first == 1:
                            dve.wait_ge(v_ones_ready, 2)
                        for kt in range(TT):
                            last = nc.vector.scalar_tensor_tensor(
                                out=v_ext[s.par(1)][:, kt, :, 0:DH],
                                in0=work[0][:, kt * HID:(kt + 1) * HID].rearrange("p (h d) -> p h d", d=DH),
                                scalar=sc_sb[:, 2:3],
                                in1=bvo_sb[:, 0, :].rearrange("p (h d) -> p h d", d=DH),
                                op0=ALU.mult, op1=ALU.add)
                        last.then_inc(v_ready, 1)
                    if t == 8 and s.has(3):
                        s.wait(dve, o_psum, 1, 3, 1)
                        s.wait(dve, y_ready, 1, 3, 1)
                        s.wait_dma(dve, out_stored, 3, later=0)
                        nc.vector.scalar_tensor_tensor(
                            out=outs[s.par(3)][:, :, :].rearrange("p t c -> p (t c)"), in0=work[1][:, 0:TT * HID],
                            scalar=sc_sb[:, 3:4], in1=y[s.par(3)][:, :, :].rearrange("p t c -> p (t c)"),
                            op0=ALU.mult, op1=ALU.add).then_inc(out_ready, 1)
                    if t == 8 and s.has(1):
                        split_max(s, 0)
                    if t == 9 and s.has(-1):
                        token_stats(s)
                    if t == 10 and s.has(-1):
                        layer_norm(s)
                    if t == 11 and s.has(1):
                        s.wait(dve, r1_hi_ready, 2, 1, 1)
                        s.wait(dve, l2_psum, 1, 2, 1)
                        relu_lo(0, work[0], r1_hi, r1_lo, r1_ready)
                    if t == 13 and s.has(1):
                        s.wait(dve, r1_hi_ready, 2, 1, 2)
                        relu_lo(1, work[1], r1_hi, r1_lo, r1_ready)
                        copy_max_rows(s, 1, 0)
                if s.has(1):
                    split_max(s, 1)

            def ffn_weights():
                n = [0]

                def link(ins):
                    n[0] += 1
                    ins.then_inc(setup_step, 1)
                    dve.wait_ge(setup_step, n[0])

                s01 = sc_sb[:, 4:6]
                dve.wait_ge(weights_loaded, 16 * N_WEIGHT_DMAS)
                nc.vector.tensor_tensor(w0d[:, :], k0_sb[:, 0, :], k0_sb[:, 1, :], ALU.subtract)
                nc.vector.tensor_scalar(sgn[:, 0:2], s01, 0.0, None, ALU.is_gt)
                link(nc.vector.tensor_scalar(sgn[:, 2:4], s01, 0.0, None, ALU.is_lt))
                link(nc.vector.tensor_tensor(sgn[:, 0:2], sgn[:, 0:2], sgn[:, 2:4], ALU.subtract))
                nc.vector.tensor_scalar(sgn[:, 4:5], sgn[:, 0:1], W0_DOWN, None, ALU.mult)
                nc.vector.tensor_scalar(sgn[:, 5:6], sgn[:, 1:2], 2.0 * W1_DOWN, None, ALU.mult)
                nc.vector.tensor_scalar(sgn[:, 6:7], sgn[:, 1:2], -W1_DOWN, None, ALU.mult)
                link(nc.vector.tensor_tensor(sgn[:, 2:4], sgn[:, 0:2], s01, ALU.mult))
                nc.vector.tensor_scalar(w0[:, :], w0d[:, :], sgn[:, 4:5], None, ALU.mult)
                nc.vector.tensor_scalar(w1[:, :, :], k1_sb[:, :, :], sgn[:, 5:6], sgn[:, 6:7], ALU.mult, ALU.add)
                nc.vector.tensor_scalar(w2[:, :, :], k2_sb[:, :, :], 2.0, -1.0, ALU.mult, ALU.add)
                link(nc.vector.scalar_tensor_tensor(out=ffn_scale[:, :], in0=sgn[:, 2:3], scalar=FFN_SCALE,
                                                    in1=sgn[:, 3:4], op0=ALU.mult, op1=ALU.mult))
                nc.vector.tensor_tensor(ffn_scale[:, :], ffn_scale[:, :], sc_sb[:, 6:7], ALU.mult
                                        ).then_inc(ffn_weights_ready, 1)

            nc.vector.memset(max_part[:, :, :], 0.0).then_inc(max_part_zeroed, 1)
            dve.wait_ge(max_part_zeroed, 1)
            run_steps(dve, step)

        @block.tensor
        def _(pe):
            mm = nc.tensor.matmul

            USERS = {0: [("l0a", 1, r0_ready, 2, 1), ("qk", 0, qk_scaled, 2, 2), ("max1", 2, max_rows_ready, 2, 2),
                         ("turn1", 3, ctxn_ready, 2, 2), ("v", 1, v_ready, 1, 1), ("l1a", 1, r1_ready, 2, 1),
                         ("max0", 1, max_rows_ready, 2, 1)],
                     1: [("xT", 0, xT_split, 1, 1), ("l0b", 1, r0_ready, 2, 2), ("turn0", 3, ctxn_ready, 2, 1),
                         ("ctxT", 3, ctxT_ready, 1, 1), ("o", 3, out_ready, 1, 1), ("l1b", 1, r1_ready, 2, 2),
                         ("l2", 1, y_ready, 1, 1)]}

            def take_bank(s, b, name):
                order = [u[0] for u in USERS[b]]
                at = order.index(name)
                for back in range(1, len(order) + 1):
                    _, lag, done, per_batch, k = USERS[b][(at - back) % len(order)]
                    lag += 1 if back > at else 0
                    if s.has(lag):
                        s.wait(pe, done, per_batch, lag, k)
                        break
                return work[b]

            def scores_for_exp(s, t):
                if t % HALF == 0:
                    s.wait(pe, max_rows_loaded[t // HALF], 16, 2, 16)
                s.wait(pe, probs_ready, HEADS, 2, t - 1)
                q, k = q_rows[s.par(2)], k_rows[s.par(2)]
                for kt in range(TT):
                    c = t * SEQ + kt * P
                    last = mm(st_bank[t % 2][:, kt * SEQ:(kt + 1) * SEQ], k[0:MROWS, c:c + P],
                              q[0:MROWS, t * SEQ:(t + 1) * SEQ], start=True, stop=True)
                last.then_inc(st_psum, 1)

            def scores_for_max(s, t):
                if t % HALF == 0:
                    s.wait(pe, rows_loaded[t // HALF], LOADS, 1, LOADS)
                s.wait(pe, max_ready, HEADS, 1, t - 1)
                q, k = q_rows[s.par(1)], k_rows[s.par(1)]
                for qt in range(TT):
                    c = t * SEQ + qt * P
                    last = mm(s_bank[t % 2][:, qt * SEQ:(qt + 1) * SEQ], q[0:ROWS, c:c + P],
                              k[0:ROWS, t * SEQ:(t + 1) * SEQ], start=True, stop=True)
                last.then_inc(s_psum, 1)

            def context(s, lag, g):
                s.wait(pe, probs_ready, HEADS, lag, GROUP * (g + 1))
                s.wait(pe, ctx_copied, GROUPS, lag, g)
                if g == 0:
                    s.wait(pe, v_ready, 1, lag, 1)
                for kt in range(TT):
                    for j in range(GROUP):
                        last = mm(ctx_bank[VC * j:VC * (j + 1), 0:SEQ], v_ext[s.par(lag)][:, kt, GROUP * g + j, :],
                                  probs[g % 2][:, j, kt, :], start=kt == 0, stop=kt == TT - 1)
                last.then_inc(ctx_psum, 1)

            def max_to_rows(s, lag, half):
                s.wait(pe, max_parts_ready, 2, lag, half + 1)
                b = take_bank(s, 0, f"max{half}")[:, :].bitcast(bf16)
                nc.tensor.transpose(b[:, 0:P], max_part[:, half, :], ident16[:, :]).then_inc(maxT_psum, 1)

            def layer0(s, k, b):
                for m in range(2):
                    c = (2 * k + m) * P
                    for n, part in enumerate((xT_hi, xT_lo)):
                        last = mm(b[:, m * SEQ:(m + 1) * SEQ], w0[:, c:c + P], part[s.par(1)][:, :],
                                  start=n == 0, stop=n == 1)
                last.then_inc(l0_psum, 1)

            def layer1_block(b, m):
                for kk in range(FB):
                    for n, part in enumerate((r0_hi, r0_lo)):
                        last = mm(b[:, (m % 2) * SEQ:(m % 2 + 1) * SEQ], w1[:, kk, m * P:(m + 1) * P],
                                  part[:, kk, :], start=kk == n == 0, stop=kk == FB - 1 and n == 1)
                return last

            def layer2_tile(b, t):
                for kk in range(FB):
                    for n, part in enumerate((r1_hi, r1_lo)):
                        last = mm(b[:, t * HID:(t + 1) * HID], part[:, kk, t * P:(t + 1) * P], w2[:, kk, :],
                                  start=kk == n == 0, stop=kk == FB - 1 and n == 1)
                return last

            def turn_context(s, q):
                b = take_bank(s, (q + 1) % 2, f"turn{q}")
                for g in range(GROUPS):
                    last = nc.tensor.transpose(b[:, g * P:(g + 1) * P], ctx_sb[:, g, q * P:(q + 1) * P], ident[:, :])
                last.then_inc(ctx_turned, 1)

            def step(s):
                for t in range(HEADS):
                    if s.has(2):
                        scores_for_exp(s, t)
                    if s.has(1):
                        scores_for_max(s, t)
                    if t == 0 and s.has(1):
                        if s.first == 1:
                            pe.wait_ge(ffn_weights_ready, 1)
                        s.wait(pe, xT_split, 1, 1, 1)
                        layer0(s, 0, take_bank(s, 0, "l0a"))
                    if t == 0 and s.has(0):
                        s.wait(pe, xn_ready, 1, 0, 1)
                        b = take_bank(s, 1, "xT")
                        for tt in range(TT):
                            last = nc.tensor.transpose(b[:, tt * P:(tt + 1) * P], xn[:, tt, :], ident[:, :])
                        last.then_inc(xT_psum, 1)
                    if t == 1 and s.has(3):
                        context(s, 3, GROUPS - 1)
                    if t == 2 and s.has(0):
                        s.wait(pe, xT_copied, 2, 0, 1)
                        b = take_bank(s, 0, "qk")
                        for n in range(2):
                            last = mm(b[:, n * SEQ:(n + 1) * SEQ], w_sb[:, n, :], xT[s.par(0)][:, :],
                                      start=True, stop=True)
                        last.then_inc(qk_psum, 1)
                    if t == 3 and s.has(1):
                        layer0(s, 1, take_bank(s, 1, "l0b"))
                    if t == 3 and s.has(2):
                        max_to_rows(s, 2, 1)
                    if t == 4 and s.has(3):
                        s.wait(pe, ctx_copied, GROUPS, 3, GROUPS)
                        for q in range(TT):
                            turn_context(s, q)
                    if t == 5 and s.has(2):
                        context(s, 2, 0)
                    if t == 6 and s.has(3):
                        s.wait(pe, ctxn_ready, TT, 3, TT)
                        b = take_bank(s, 1, "ctxT")
                        for q in range(TT):
                            last = nc.tensor.transpose(b[:, q * P:(q + 1) * P], ctxn[:, q, :], ident[:, :])
                        last.then_inc(ctxT_psum, 1)
                    if t == 6 and s.has(1):
                        b = take_bank(s, 0, "v")
                        for kt in range(TT):
                            last = mm(b[:, kt * HID:(kt + 1) * HID], xT[s.par(1)][:, kt * P:(kt + 1) * P],
                                      w_sb[:, 2, :], start=True, stop=True)
                        last.then_inc(v_psum, 1)
                    if t == 7 and s.has(3):
                        s.wait(pe, ctxT_ready, 1, 3, 1)
                        b = take_bank(s, 1, "o")
                        for q in range(TT):
                            last = mm(b[:, q * HID:(q + 1) * HID], ctxT[:, q * P:(q + 1) * P], w_sb[:, 3, :],
                                      start=True, stop=True)
                        last.then_inc(o_psum, 1)
                    if t == 8 and s.has(1):
                        s.wait(pe, r0_ready, 2, 1, 2)
                        layer1_block(take_bank(s, 0, "l1a"), 0)
                    if t == 9 and s.has(2):
                        context(s, 2, 1)
                    if t == 10 and s.has(1):
                        layer1_block(work[0], 1).then_inc(l1_psum, 1)
                    if t == 11 and s.has(1):
                        layer1_block(take_bank(s, 1, "l1b"), 2)
                    if t == 12 and s.has(1):
                        layer1_block(work[1], 3).then_inc(l1_psum, 1)
                        max_to_rows(s, 1, 0)
                    if t == 13 and s.has(2):
                        context(s, 2, 2)
                    if t == 14 and s.has(1):
                        s.wait(pe, r1_ready, 2, 1, 2)
                        layer2_tile(take_bank(s, 1, "l2"), 0)
                    if t == 15 and s.has(1):
                        layer2_tile(work[1], 1).then_inc(l2_psum, 1)

            pe.wait_ge(ident_ready, 2)
            pe.wait_ge(weights_loaded, 16 * N_WEIGHT_DMAS)
            run_steps(pe, step)


def kernel(L0_attn_x, L0_attn_w_q, L0_attn_s_q, L0_attn_b_q, L0_attn_w_k, L0_attn_s_k, L0_attn_b_k,
           L0_attn_w_v, L0_attn_s_v, L0_attn_b_v, L0_attn_w_o, L0_attn_s_o, L0_attn_b_o,
           L0_ffn_k0, L0_ffn_k1, L0_ffn_k2, L0_ffn_s0, L0_ffn_s1, L0_ffn_s2):
    import numpy as np
    import concourse.bacc as bacc
    from concourse.bass_utils import run_bass_kernel_spmd

    def by_half_dim_head(a):
        a = np.asarray(a)
        return np.swapaxes(a.reshape(a.shape[:-1] + (2, HALF, DH)), -1, -2).reshape(a.shape)

    w4 = np.stack([by_half_dim_head(np.asarray(L0_attn_w_q).T), by_half_dim_head(np.asarray(L0_attn_w_k).T),
                   np.asarray(L0_attn_w_v).T, np.asarray(L0_attn_w_o).T], axis=1)
    arrays = {
        "x": np.asarray(L0_attn_x),
        "w4": w4,
        "bqk": np.stack([by_half_dim_head(L0_attn_b_q), by_half_dim_head(L0_attn_b_k)], axis=1),
        "bvo": np.concatenate([np.asarray(L0_attn_b_v), np.asarray(L0_attn_b_o)])[None, :],
        "sc7": np.stack([np.asarray(v).reshape(()) for v in (
            L0_attn_s_q, L0_attn_s_k, L0_attn_s_v, L0_attn_s_o, L0_ffn_s0, L0_ffn_s1, L0_ffn_s2)])[None, :],
        "k0": np.ascontiguousarray(L0_ffn_k0).view(np.uint32),
        "k1": np.ascontiguousarray(L0_ffn_k1).view(np.uint32),
        "k2": np.ascontiguousarray(L0_ffn_k2).view(np.uint32),
    }
    arrays = {n: np.ascontiguousarray(a) for n, a in arrays.items()}
    nc = bacc.Bacc("TRN2", target_bir_lowering=False, num_devices=1)
    args = [nc.dram_tensor(n, a.shape, mybir.dt.from_np(a.dtype), kind="ExternalInput").ap()
            for n, a in arrays.items()]
    out = nc.dram_tensor("out", (BATCH, SEQ, HID), mybir.dt.float32, kind="ExternalOutput").ap()
    build(nc, *args, out)
    r = run_bass_kernel_spmd(nc, [arrays], core_ids=[0])
    return r.results[0]["out"]
```

```python
from contextlib import ExitStack

import concourse.bass as bass
from concourse import mybir

BATCH, SEQ, HID = 16, 256, 128
HEADS, DH = 16, 8
HALF = HEADS // 2
FEAT = 512
P = 128
TT = SEQ // P
FB = FEAT // P
PARTS = 3
ROWS = DH * PARTS * PARTS
MROWS = ROWS + PARTS
GROUP = 4
GROUPS = HEADS // GROUP
VC = 32
EPS = 1e-5
EXP_SCALE = float(DH) ** -0.5
X_UP = 2.0 ** 12
W0_DOWN = 2.0 ** -4
W1_DOWN = 2.0 ** -9
FFN_SCALE = 2.0 * 2.0 * 2.0 / (X_UP * W0_DOWN * W1_DOWN)
LOOP_FIRST, LOOP_STEPS = 3, 12
LAST_STEP = BATCH + 2


class Step:

    def __init__(self, first, loop=None):
        self.first, self.loop = first, loop

    def count(self, per_step, const):
        if self.loop is None:
            return per_step * self.first + const
        return self.loop * (2 * per_step) + (per_step * self.first + const)

    def has(self, lag):
        return self.loop is not None or 0 <= self.first - lag < BATCH

    def batch(self, lag):
        return self.count(1, -lag)

    def par(self, lag):
        return (self.first - lag) % 2

    def wait(self, eng, sem, per_batch, lag, k):
        v = self.count(per_batch, k - per_batch * lag)
        if self.loop is not None or v > 0:
            eng.wait_ge(sem, v)

    def wait_dma(self, eng, sems, lag, later=1):
        q = self.par(lag)
        v = self.count(8, -8 * lag - 8 * q + 16 * later)
        if self.loop is not None or v > 0:
            eng.wait_ge(sems[q], v)


def run_steps(eng, step):
    for i in range(-1, LOOP_FIRST):
        step(Step(i))
    with eng.Fori(0, LOOP_STEPS // 2) as it:
        step(Step(LOOP_FIRST, it))
        step(Step(LOOP_FIRST + 1, it))
    for i in range(LOOP_FIRST + LOOP_STEPS, LAST_STEP + 1):
        step(Step(i))


def build(nc, x, w4, bqkv, bo, sc7, k0, k1, k2, out):
    f32, bf16, f16, u8 = mybir.dt.float32, mybir.dt.bfloat16, mybir.dt.float16, mybir.dt.uint8
    ALU, ACT, AX = mybir.AluOpType, mybir.ActivationFunctionType, mybir.AxisListType

    q_scratch = nc.dram_tensor("q_scratch", (2, PARTS * DH, HALF, SEQ), bf16, kind="Internal").ap()
    k_scratch = nc.dram_tensor("k_scratch", (2, DH * PARTS, HALF, SEQ), bf16, kind="Internal").ap()

    with ExitStack() as ctx:
        def sb(name, shape, dt):
            return ctx.enter_context(nc.sbuf_tensor(name, shape, dt))

        def sem(name):
            return ctx.enter_context(nc.semaphore(name))

        w_sb = sb("w_sb", [P, 4, HID], f32)
        bqkv_sb = sb("bqkv_sb", [P, 3], f32)
        bo_sb = sb("bo_sb", [P, 1, HID], f32)
        sc_sb = sb("sc_sb", [P, 7], f32)
        k0_sb = sb("k0_sb", [P, 2, FEAT], u8)
        k1_sb = sb("k1_sb", [P, FB, FEAT], u8)
        k2_sb = sb("k2_sb", [P, FB, HID], u8)
        w0d = sb("w0d", [P, FEAT], f16)
        w0 = sb("w0", [P, FEAT], f16)
        w1 = sb("w1", [P, FB, FEAT], f16)
        w2 = sb("w2", [P, FB, HID], f16)
        sgn = sb("sgn", [P, 8], f32)
        ffn_scale = sb("ffn_scale", [P, 1], f32)
        ident = sb("ident", [P, P], f32)
        ident16 = sb("ident16", [P, P], bf16)
        xin = [sb(f"xin{n}", [P, TT, HID], f32) for n in range(2)]
        stats = sb("stats", [P, TT, 6], f32)
        meanvar = sb("meanvar", [P, TT, 2], f32)
        var_eps = sb("var_eps", [P, TT], f32)
        eps = sb("eps", [P, TT], f32)
        minus_half = sb("minus_half", [P, TT], f32)
        rstd = sb("rstd", [P, TT], f32)
        xn = sb("xn", [P, TT, HID], f32)
        xres = [sb(f"xres{n}", [P, TT, HID], f32) for n in range(2)]
        xT = [sb(f"xT{n}", [P, SEQ], f32) for n in range(2)]
        xT_hi = [sb(f"xT_hi{n}", [P, SEQ], f16) for n in range(2)]
        xT_lo = [sb(f"xT_lo{n}", [P, SEQ], f16) for n in range(2)]
        qk = sb("qk", [P, 2, SEQ], f32)
        qk_rest = sb("qk_rest", [P, 2, SEQ], f32)
        qk_part = sb("qk_part", [P, PARTS, 2, SEQ], bf16)
        q_rows = [sb(f"q_rows{n}", [P, HEADS * SEQ], bf16) for n in range(2)]
        k_rows = [sb(f"k_rows{n}", [P, HEADS * SEQ], bf16) for n in range(2)]
        neg_max = sb("neg_max", [P, 2, HALF, TT], f32)
        max_rest = sb("max_rest", [P, 2, HALF * TT], f32)
        max_part = sb("max_part", [P, 2, P], bf16)
        max_rows = [sb(f"max_rows{n}", [PARTS * HALF * TT, P], bf16) for n in range(2)]
        v_ext = [sb(f"v_ext{n}", [P, TT, HEADS, VC], f32) for n in range(2)]
        r0_hi = sb("r0_hi", [P, FB, SEQ], f16)
        r0_lo = sb("r0_lo", [P, FB, SEQ], f16)
        r1_hi = sb("r1_hi", [P, FB, SEQ], f16)
        r1_lo = sb("r1_lo", [P, FB, SEQ], f16)
        y = [sb(f"y{n}", [P, TT, HID], f32) for n in range(2)]
        probs = [sb(f"probs{n}", [P, GROUP, TT, SEQ], f32) for n in range(2)]
        ctx_sb = sb("ctx_sb", [P, GROUPS, SEQ], f32)
        rden = sb("rden", [P, TT, HEADS], f32)
        ctxn = sb("ctxn", [P, TT, HID], f32)
        ctxT = sb("ctxT", [P, SEQ], f32)
        outs = [sb(f"outs{n}", [P, TT, HID], f32) for n in range(2)]

        def bank(name):
            return ctx.enter_context(nc.psum_tensor(name, [P, 2 * SEQ], f32))

        s_bank = [bank(f"s_bank{n}") for n in range(2)]
        st_bank = [bank(f"st_bank{n}") for n in range(2)]
        ctx_bank = bank("ctx_bank")
        work = [bank(f"work{n}") for n in range(3)]
        BANK = {"l0a": 0, "qk": 0, "l1a": 0, "o": 0,
                "l0b": 1, "turn1": 1, "l1b": 1, "l2": 1,
                "xT": 2, "max1": 2, "turn0": 2, "ctxT": 2, "max0": 2, "v": 2}

        def psum(name):
            return work[BANK[name]]


        weights_loaded = sem("weights_loaded")
        x_loaded = [sem(f"x_loaded{n}") for n in range(2)]
        k_stored = sem("k_stored")
        q_stored = [sem(f"q_stored{h}") for h in range(2)]
        rows_loaded = [sem(f"rows_loaded{n}") for n in range(2)]
        max_rows_loaded = [sem(f"max_rows_loaded{n}") for n in range(2)]
        out_stored = [sem(f"out_stored{n}") for n in range(2)]
        ident_zeroed = sem("ident_zeroed")
        ident_ready = sem("ident_ready")
        ones_ready = sem("ones_ready")
        v_zeroed = sem("v_zeroed")
        v_ones_ready = sem("v_ones_ready")
        setup_step = sem("setup_step")
        ffn_weights_ready = sem("ffn_weights_ready")
        ln_step = sem("ln_step")
        half_ready = sem("half_ready")
        meanvar_ready = sem("meanvar_ready")
        ln_pool_step = sem("ln_pool_step")
        xn_ready = sem("xn_ready")
        xres_ready = sem("xres_ready")
        xT_psum = sem("xT_psum")
        xT_copied = sem("xT_copied")
        xT_split = sem("xT_split")
        qk_psum = sem("qk_psum")
        qk_scaled = sem("qk_scaled")
        qk_hi_ready = sem("qk_hi_ready")
        qk_rest_ready = sem("qk_rest_ready")
        qk_mid_ready = sem("qk_mid_ready")
        parts_ready = sem("parts_ready")
        s_psum = sem("s_psum")
        max_ready = sem("max_ready")
        max_split_step = sem("max_split_step")
        max_part_zeroed = sem("max_part_zeroed")
        max_parts_ready = sem("max_parts_ready")
        maxT_psum = sem("maxT_psum")
        max_rows_ready = sem("max_rows_ready")
        v_psum = sem("v_psum")
        v_ready = sem("v_ready")
        l0_psum = sem("l0_psum")
        r0_hi_ready = sem("r0_hi_ready")
        r0_ready = sem("r0_ready")
        l1_psum = sem("l1_psum")
        r1_hi_ready = sem("r1_hi_ready")
        r1_ready = sem("r1_ready")
        l2_psum = sem("l2_psum")
        y_ready = sem("y_ready")
        st_psum = sem("st_psum")
        probs_ready = sem("probs_ready")
        ctx_psum = sem("ctx_psum")
        ctx_copied = sem("ctx_copied")
        ctx_turned = sem("ctx_turned")
        rden_ready = sem("rden_ready")
        ctxn_ready = sem("ctxn_ready")
        ctxT_psum = sem("ctxT_psum")
        ctxT_ready = sem("ctxT_ready")
        o_psum = sem("o_psum")
        out_ready = sem("out_ready")

        N_WEIGHT_DMAS = 7
        LOADS = 16 * 2
        block = ctx.enter_context(nc.Block())

        @block.sync
        def _(sp):
            def step(s):
                load_batch = sp.snap(s.batch(-1)) if s.loop is not None else s.batch(-1)
                store_batch = sp.snap(s.batch(3)) if s.loop is not None else s.batch(3)
                rows_free = [s.count(HEADS, HALF * (h + 1) - 2 * HEADS) for h in range(2)]
                rows_read = s.count(LOADS, 0)
                if s.loop is not None:
                    rows_read = sp.snap(sp.to_reg(rows_read))
                    rows_free = [sp.snap(sp.to_reg(v)) for v in rows_free]
                if s.has(2):
                    s.wait(sp, max_rows_ready, 2, 2, 2)
                    sp.dma_start(q_rows[s.par(2)][ROWS:MROWS, HALF * SEQ:], max_rows[1][:, :]
                                 ).then_inc(max_rows_loaded[1], 16)
                if s.has(-1):
                    s.wait(sp, xn_ready, 1, 1, 1)
                    s.wait(sp, xres_ready, 1, 1, 1)
                    sp.dma_start(xin[s.par(-1)][:, :, :],
                                 x[bass.ds(load_batch, 1), :, :].rearrange("a (t p) c -> p (a t) c", p=P)
                                 ).then_inc(x_loaded[s.par(-1)], 16)
                if s.first == -1:
                    load_weights()
                if s.has(0):
                    k_dst = k_scratch.rearrange("h (d r) e t -> r (h d) e t", r=PARTS)
                    for r, ready in enumerate((qk_hi_ready, qk_mid_ready, parts_ready)):
                        s.wait(sp, ready, 1, 0, 1)
                        if r == 0 and s.has(1):
                            for h in range(2):
                                sp.wait_ge(rows_loaded[h], rows_read)
                        sp.dma_start(k_dst[r], qk_part[:, r, 1, :]).then_inc(k_stored, 16)
                    for h in range(2):
                        sp.dma_start(q_scratch[h].rearrange("(r d) e t -> (d e) r t", r=PARTS),
                                     qk_part[h * P // 2:(h + 1) * P // 2, :, 0, :]).then_inc(q_stored[h], 16)
                for h in range(2):
                    if h == 1 and s.has(1):
                        s.wait(sp, max_rows_ready, 2, 1, 1)
                        sp.dma_start(q_rows[s.par(1)][ROWS:MROWS, :HALF * SEQ], max_rows[0][:, :]
                                     ).then_inc(max_rows_loaded[0], 16)
                    if h == 1 and s.has(3):
                        s.wait(sp, out_ready, 1, 3, 1)
                        sp.dma_start(out[bass.ds(store_batch, 1), :, :].rearrange("a (t p) c -> p (a t) c", p=P),
                                     outs[s.par(3)][:, :, :]).then_inc(out_stored[s.par(3)], 16)
                    if s.has(0):
                        cols = slice(h * HALF * SEQ, (h + 1) * HALF * SEQ)
                        if h == 0:
                            s.wait(sp, k_stored, 16 * PARTS, 0, 16 * PARTS)
                        if s.has(2):
                            sp.wait_ge(st_psum, rows_free[h])
                        if s.first == 0 and h == 0:
                            sp.wait_ge(ones_ready, 2)
                        k_src = k_scratch[h:h + 1].rearrange("x r e t -> x r (e t)")
                        sp.dma_start(k_rows[s.par(0)][0:ROWS, cols],
                                     k_src.to_broadcast([PARTS, DH * PARTS, HALF * SEQ])
                                     ).then_inc(rows_loaded[h], 16)
                        s.wait(sp, q_stored[h], 16, 0, 16)
                        q_src = q_scratch[h].rearrange("(r x) e t -> r x (e t)", x=1)
                        sp.dma_start(q_rows[s.par(0)][0:ROWS, cols],
                                     q_src.to_broadcast([PARTS * DH, PARTS, HALF * SEQ])
                                     ).then_inc(rows_loaded[h], 16)

            def load_weights():
                for dst, src in ((w_sb[:, :, :], w4), (bqkv_sb[:, :], bqkv),
                                 (sc_sb[:, :], sc7.to_broadcast([P, 7])),
                                 (bo_sb[:, 0, :], bo.to_broadcast([P, HID])),
                                 (k0_sb[:, :, :].bitcast(mybir.dt.uint32), k0.rearrange("(a p) f -> p a f", p=P)),
                                 (k1_sb[:, :, :].bitcast(mybir.dt.uint32), k1.rearrange("(a p) f -> p a f", p=P)),
                                 (k2_sb[:, :, :].bitcast(mybir.dt.uint32), k2.rearrange("(a p) f -> p a f", p=P))):
                    sp.dma_start(dst, src).then_inc(weights_loaded, 16)

            run_steps(sp, step)
            for n in range(2):
                sp.wait_ge(out_stored[n], 16 * BATCH // 2)

        @block.gpsimd
        def _(pool):
            def step(s):
                if s.has(0):
                    residual_and_parts(s)
                if s.has(-1):
                    s.wait(pool, meanvar_ready, TT, -1, TT)
                    nc.gpsimd.tensor_tensor(var_eps[:, :], meanvar[:, :, 1], eps[:, :], ALU.add
                                            ).then_inc(ln_pool_step, 1)
                    s.wait(pool, xT_psum, 1, 0, 1)
                    nc.gpsimd.tensor_tensor(xn[:, :, :], xin[s.par(-1)][:, :, :],
                                            meanvar[:, :, 0:1].to_broadcast([P, TT, HID]), ALU.subtract
                                            ).then_inc(ln_pool_step, 1)
                    s.wait(pool, ln_pool_step, 3, -1, 2)
                    nc.gpsimd.tensor_tensor(rstd[:, :], var_eps[:, :], minus_half[:, :], ALU.pow
                                            ).then_inc(ln_pool_step, 1)
                    s.wait(pool, ln_pool_step, 3, -1, 3)
                    nc.gpsimd.tensor_tensor(xn[:, :, :], xn[:, :, :],
                                            rstd[:, :].unsqueeze(2).to_broadcast([P, TT, HID]), ALU.mult
                                            ).then_inc(xn_ready, 1)
                if s.first == 0:
                    for n in range(2):
                        nc.gpsimd.memset(v_ext[n][:, :, :, :], 0.0).then_inc(v_zeroed, 1)
                    pool.wait_ge(v_zeroed, 2)
                    for n in range(2):
                        nc.gpsimd.memset(v_ext[n][:, :, :, DH:DH + 1], 1.0).then_inc(v_ones_ready, 1)

            def residual_and_parts(s):
                if s.first == 0:
                    pool.wait_ge(weights_loaded, 16 * N_WEIGHT_DMAS)
                s.wait_dma(pool, x_loaded, 0)
                s.wait(pool, y_ready, 1, 2, 1)
                nc.gpsimd.tensor_tensor(xres[s.par(0)][:, :, :], xin[s.par(0)][:, :, :],
                                        bo_sb[:, :, :].to_broadcast([P, TT, HID]), ALU.add
                                        ).then_inc(xres_ready, 1)
                s.wait(pool, qk_hi_ready, 1, 0, 1)
                nc.gpsimd.tensor_tensor(qk_rest[:, :, :], qk[:, :, :], qk_part[:, 0], ALU.subtract
                                        ).then_inc(qk_rest_ready, 1)
                s.wait(pool, qk_mid_ready, 1, 0, 1)
                nc.gpsimd.tensor_tensor(qk_part[:, 2], qk_rest[:, :, :], qk_part[:, 1], ALU.subtract
                                        ).then_inc(parts_ready, 1)

            nc.gpsimd.memset(minus_half[:, :], -0.5).then_inc(half_ready, 1)
            nc.gpsimd.memset(eps[:, :], EPS).then_inc(half_ready, 1)
            pool.wait_ge(half_ready, 2)
            nc.gpsimd.memset(ident[:, :], 0.0).then_inc(ident_zeroed, 1)
            nc.gpsimd.memset(ident16[:, :], 0.0).then_inc(ident_zeroed, 1)
            pool.wait_ge(ident_zeroed, 2)
            for m in (ident, ident16):
                nc.gpsimd.affine_select(out=m[:, :], in_=m[:, :], compare_op=ALU.not_equal, fill=1.0, base=0,
                                        pattern=[[-1, P]], channel_multiplier=1).then_inc(ident_ready, 1)
            run_steps(pool, step)

        @block.scalar
        def _(act):
            def context_copy(s, lag, g):
                s.wait(act, ctx_psum, GROUPS, lag, g + 1)
                if g == 0:
                    s.wait(act, ctx_turned, TT, lag + 1, TT)
                nc.scalar.activation(ctx_sb[:, g, :], ctx_bank[:, 0:SEQ], ACT.Copy).then_inc(ctx_copied, 1)

            def relu_hi(k, b, dst, ready):
                nc.scalar.activation(dst[:, 2 * k:2 * k + 2, :].rearrange("p m t -> p (m t)"), b[:, :],
                                     ACT.Relu).then_inc(ready, 1)

            def step(s):
                for t in range(HEADS):
                    if s.has(2):
                        s.wait(act, st_psum, HEADS, 2, t + 1)
                        if t % GROUP == 0:
                            s.wait(act, ctx_psum, GROUPS, 2, t // GROUP - 1)
                        nc.scalar.activation(
                            probs[t // GROUP % 2][:, t % GROUP, :, :].rearrange("p k q -> p (k q)"),
                            st_bank[t % 2][:, :], ACT.Exp, scale=EXP_SCALE).then_inc(probs_ready, 1)
                    if t == 1 and s.has(0):
                        s.wait(act, xT_psum, 1, 0, 1)
                        s.wait(act, v_psum, 1, 2, 1)
                        s.wait(act, l0_psum, 2, 2, 2)
                        b = psum("xT")[:, 0:SEQ]
                        nc.scalar.activation(xT[s.par(0)][:, :], b, ACT.Copy).then_inc(xT_copied, 1)
                        nc.scalar.activation(xT_hi[s.par(0)][:, :], b, ACT.Copy, scale=X_UP).then_inc(xT_copied, 1)
                    if t == 1 and s.has(1):
                        s.wait(act, l0_psum, 2, 1, 1)
                        s.wait(act, l1_psum, 2, 2, 2)
                        relu_hi(0, psum("l0a"), r0_hi, r0_hi_ready)
                    if t == 2 and s.has(3):
                        context_copy(s, 3, GROUPS - 1)
                    if t == 3 and s.has(1):
                        s.wait(act, l0_psum, 2, 1, 2)
                        relu_hi(1, psum("l0b"), r0_hi, r0_hi_ready)
                    if t == 5 and s.has(0):
                        s.wait(act, qk_psum, 1, 0, 1)
                        s.wait(act, parts_ready, 1, 1, 1)
                        s.wait(act, k_stored, 16 * PARTS, 1, 16 * PARTS)
                        for h in range(2):
                            s.wait(act, q_stored[h], 16, 1, 16)
                        for n in range(2):
                            nc.scalar.activation(qk[:, n, :], psum("qk")[:, n * SEQ:(n + 1) * SEQ], ACT.Identity,
                                                 scale=sc_sb[:, n:n + 1], bias=bqkv_sb[:, n:n + 1]
                                                 ).then_inc(qk_scaled, 1)
                        s.wait(act, qk_scaled, 2, 0, 2)
                        nc.scalar.activation(qk_part[:, 0], qk[:, :, :], ACT.Copy).then_inc(qk_hi_ready, 1)
                    if t == 6 and s.has(2):
                        context_copy(s, 2, 0)
                    if t == 6 and s.has(0):
                        s.wait(act, qk_rest_ready, 1, 0, 1)
                        nc.scalar.activation(qk_part[:, 1], qk_rest[:, :, :], ACT.Copy).then_inc(qk_mid_ready, 1)
                    if t == 8 and s.has(1):
                        s.wait(act, l1_psum, 2, 1, 1)
                        s.wait(act, l2_psum, 1, 2, 1)
                        relu_hi(0, psum("l1a"), r1_hi, r1_hi_ready)
                    if t == 9 and s.has(3):
                        s.wait(act, ctxT_psum, 1, 3, 1)
                        s.wait(act, o_psum, 1, 4, 1)
                        nc.scalar.activation(ctxT[:, :], psum("ctxT")[:, 0:SEQ], ACT.Identity, scale=sc_sb[:, 2:3],
                                             bias=bqkv_sb[:, 2:3]).then_inc(ctxT_ready, 1)
                    if t == 10 and s.has(2):
                        context_copy(s, 2, 1)
                    if t == 11 and s.has(1):
                        s.wait(act, l1_psum, 2, 1, 2)
                        relu_hi(1, psum("l1b"), r1_hi, r1_hi_ready)
                    if t == 13 and s.has(1):
                        s.wait(act, v_psum, 1, 1, 1)
                        s.wait(act, ctx_psum, GROUPS, 3, GROUPS)
                        if s.first == 1:
                            act.wait_ge(v_ones_ready, 2)
                        nc.scalar.activation(
                            v_ext[s.par(1)][:, :, :, 0:DH],
                            psum("v")[:, 0:TT * HID].rearrange("p (t h d) -> p t h d", t=TT, d=DH), ACT.Copy
                        ).then_inc(v_ready, 1)
                    if t == 14 and s.has(2):
                        context_copy(s, 2, 2)

            act.wait_ge(weights_loaded, 16 * N_WEIGHT_DMAS)
            run_steps(act, step)

        @block.vector
        def _(dve):
            def token_stats(s):
                s.wait_dma(dve, x_loaded, -1)
                for t in range(TT):
                    nc.vector.bn_stats(stats[:, t, :], xin[s.par(-1)][:, t, :]).then_inc(ln_step, 1)

            def split_max(s, lag, half, link):
                full = neg_max[:, half, :, :].rearrange("p h t -> p (h t)")
                rest = max_rest[:, half, :]
                part = max_part[:, half, 0:PARTS * HALF * TT].rearrange("p (r c) -> p r c", r=PARTS)
                if link == 0:
                    s.wait(dve, max_ready, HEADS, lag, HALF * (half + 1))
                    s.wait(dve, maxT_psum, 2, lag + 1, half + 1)
                    nc.vector.tensor_copy(part[:, 0, :], full).then_inc(max_split_step, 1)
                elif link == 1:
                    s.wait(dve, max_split_step, 6, lag, 3 * half + 1)
                    nc.vector.tensor_tensor(rest, full, part[:, 0, :], ALU.subtract).then_inc(max_split_step, 1)
                elif link == 2:
                    s.wait(dve, max_split_step, 6, lag, 3 * half + 2)
                    nc.vector.tensor_copy(part[:, 1, :], rest).then_inc(max_split_step, 1)
                else:
                    s.wait(dve, max_split_step, 6, lag, 3 * half + 3)
                    nc.vector.tensor_tensor(part[:, 2, :], rest, part[:, 1, :], ALU.subtract
                                            ).then_inc(max_parts_ready, 1)

            def copy_max_rows(s, lag, half):
                s.wait(dve, maxT_psum, 2, lag, half + 1)
                s.wait(dve, max_rows_loaded[half], 16, lag + 1, 16)
                src = psum(f"max{half}")[:, :].bitcast(bf16)
                nc.vector.tensor_copy(max_rows[half][:, :], src[0:PARTS * HALF * TT, 0:P]
                                      ).then_inc(max_rows_ready, 1)

            def relu_lo(k, b, hi, lo, ready):
                nc.vector.scalar_tensor_tensor(
                    out=lo[:, 2 * k:2 * k + 2, :].rearrange("p m t -> p (m t)"), in0=b[:, :], scalar=0.0,
                    in1=hi[:, 2 * k:2 * k + 2, :].rearrange("p m t -> p (m t)"),
                    op0=ALU.max, op1=ALU.subtract).then_inc(ready, 1)

            def step(s):
                if s.first == 0:
                    for n in range(2):
                        nc.vector.memset(k_rows[n][64:MROWS, :], 1.0).then_inc(ones_ready, 1)
                    ffn_weights()
                for t in range(HEADS):
                    if t == 11 and s.has(-1):
                        s.wait(dve, xn_ready, 1, 0, 1)
                        s.wait(dve, ln_step, TT, -1, TT)
                    if s.has(1):
                        s.wait(dve, s_psum, HEADS, 1, t + 1)
                        nc.vector.tensor_reduce(out=neg_max[:, t // HALF, t % HALF, :],
                                                in_=s_bank[t % 2][:, :].rearrange("p (q k) -> p q k", q=TT),
                                                op=ALU.max, axis=AX.X, negate=True).then_inc(max_ready, 1)
                    if t == 0 and s.has(2):
                        split_max(s, 2, 1, 0)
                        s.wait(dve, l2_psum, 1, 2, 1)
                        s.wait(dve, xres_ready, 1, 2, 1)
                        nc.vector.scalar_tensor_tensor(
                            out=y[s.par(2)][:, :, :].rearrange("p t c -> p (t c)"), in0=psum("l2")[:, 0:TT * HID],
                            scalar=ffn_scale[:, :], in1=xres[s.par(2)][:, :, :].rearrange("p t c -> p (t c)"),
                            op0=ALU.mult, op1=ALU.add).then_inc(y_ready, 1)
                    if t in (0, 1) and s.has(2):
                        split_max(s, 2, 1, t + 1)
                    if t == 1 and s.has(0):
                        s.wait(dve, xT_copied, 2, 0, 2)
                        s.wait(dve, l0_psum, 2, 2, 2)
                        nc.vector.scalar_tensor_tensor(
                            out=xT_lo[s.par(0)][:, :], in0=psum("xT")[:, 0:SEQ], scalar=X_UP,
                            in1=xT_hi[s.par(0)][:, :], op0=ALU.mult, op1=ALU.subtract).then_inc(xT_split, 1)
                    if t == 1 and s.has(2):
                        split_max(s, 2, 1, 3)
                    if t == 2 and s.has(1):
                        s.wait(dve, r0_hi_ready, 2, 1, 1)
                        s.wait(dve, l1_psum, 2, 2, 2)
                        relu_lo(0, psum("l0a"), r0_hi, r0_lo, r0_ready)
                    if t == 4 and s.has(1):
                        s.wait(dve, r0_hi_ready, 2, 1, 2)
                        relu_lo(1, psum("l0b"), r0_hi, r0_lo, r0_ready)
                    if t == 3 and s.has(2):
                        copy_max_rows(s, 2, 1)
                    if t in (5, 7) and s.has(3):
                        divide_context(s, 0 if t == 5 else 1)
                    if t == 7 and s.has(1):
                        split_max(s, 1, 0, 0)
                        split_max(s, 1, 0, 1)
                    if t == 8 and s.has(1):
                        split_max(s, 1, 0, 2)
                        split_max(s, 1, 0, 3)
                    if t == 9 and s.has(1):
                        s.wait(dve, r1_hi_ready, 2, 1, 1)
                        s.wait(dve, l2_psum, 1, 2, 1)
                        relu_lo(0, psum("l1a"), r1_hi, r1_lo, r1_ready)
                    if t == 10 and s.has(-1):
                        token_stats(s)
                    if t == 11 and s.has(-1):
                        for tt in range(TT):
                            nc.vector.bn_aggr(meanvar[:, tt, :], stats[:, tt, :]).then_inc(meanvar_ready, 1)
                    if t == 11 and s.has(1):
                        copy_max_rows(s, 1, 0)
                    if t == 12 and s.has(1):
                        s.wait(dve, r1_hi_ready, 2, 1, 2)
                        relu_lo(1, psum("l1b"), r1_hi, r1_lo, r1_ready)
                    if t == 13 and s.has(3):
                        s.wait(dve, o_psum, 1, 3, 1)
                        s.wait(dve, y_ready, 1, 3, 1)
                        s.wait_dma(dve, out_stored, 3, later=0)
                        nc.vector.scalar_tensor_tensor(
                            out=outs[s.par(3)][:, :, :].rearrange("p t c -> p (t c)"), in0=psum("o")[:, 0:TT * HID],
                            scalar=sc_sb[:, 3:4], in1=y[s.par(3)][:, :, :].rearrange("p t c -> p (t c)"),
                            op0=ALU.mult, op1=ALU.add).then_inc(out_ready, 1)

            def divide_context(s, q):
                s.wait(dve, ctx_turned, TT, 3, q + 1)
                s.wait(dve, ctxT_psum, 1, 4, 1)
                heads = psum(f"turn{q}")[:, :].rearrange("p (h c) -> p h c", c=VC)
                nc.vector.reciprocal(rden[:, q, :], heads[:, :, DH]).then_inc(rden_ready, 1)
                s.wait(dve, rden_ready, TT, 3, q + 1)
                nc.vector.tensor_tensor(
                    ctxn[:, q, :].rearrange("p (h d) -> p h d", d=DH), heads[:, :, 0:DH],
                    rden[:, q, :].unsqueeze(2).to_broadcast([P, HEADS, DH]), ALU.mult).then_inc(ctxn_ready, 1)

            def ffn_weights():
                n = [0]

                def link(ins):
                    n[0] += 1
                    ins.then_inc(setup_step, 1)
                    dve.wait_ge(setup_step, n[0])

                s01 = sc_sb[:, 4:6]
                dve.wait_ge(weights_loaded, 16 * N_WEIGHT_DMAS)
                nc.vector.tensor_tensor(w0d[:, :], k0_sb[:, 0, :], k0_sb[:, 1, :], ALU.subtract)
                nc.vector.tensor_scalar(sgn[:, 0:2], s01, 0.0, None, ALU.is_gt)
                link(nc.vector.tensor_scalar(sgn[:, 2:4], s01, 0.0, None, ALU.is_lt))
                link(nc.vector.tensor_tensor(sgn[:, 0:2], sgn[:, 0:2], sgn[:, 2:4], ALU.subtract))
                nc.vector.tensor_scalar(sgn[:, 4:5], sgn[:, 0:1], W0_DOWN, None, ALU.mult)
                nc.vector.tensor_scalar(sgn[:, 5:6], sgn[:, 1:2], 2.0 * W1_DOWN, None, ALU.mult)
                nc.vector.tensor_scalar(sgn[:, 6:7], sgn[:, 1:2], -W1_DOWN, None, ALU.mult)
                link(nc.vector.tensor_tensor(sgn[:, 2:4], sgn[:, 0:2], s01, ALU.mult))
                nc.vector.tensor_scalar(w0[:, :], w0d[:, :], sgn[:, 4:5], None, ALU.mult)
                nc.vector.tensor_scalar(w1[:, :, :], k1_sb[:, :, :], sgn[:, 5:6], sgn[:, 6:7], ALU.mult, ALU.add)
                nc.vector.tensor_scalar(w2[:, :, :], k2_sb[:, :, :], 2.0, -1.0, ALU.mult, ALU.add)
                link(nc.vector.scalar_tensor_tensor(out=ffn_scale[:, :], in0=sgn[:, 2:3], scalar=FFN_SCALE,
                                                    in1=sgn[:, 3:4], op0=ALU.mult, op1=ALU.mult))
                nc.vector.tensor_tensor(ffn_scale[:, :], ffn_scale[:, :], sc_sb[:, 6:7], ALU.mult
                                        ).then_inc(ffn_weights_ready, 1)

            nc.vector.memset(max_part[:, :, :], 0.0).then_inc(max_part_zeroed, 1)
            dve.wait_ge(max_part_zeroed, 1)
            run_steps(dve, step)

        @block.tensor
        def _(pe):
            mm = nc.tensor.matmul

            USERS = [("l0a", 1, r0_ready, 2, 1), ("xT", 0, xT_split, 1, 1), ("l0b", 1, r0_ready, 2, 2),
                     ("max1", 2, max_rows_ready, 2, 2), ("qk", 0, qk_scaled, 2, 2),
                     ("turn0", 3, ctxn_ready, 2, 1), ("turn1", 3, ctxn_ready, 2, 2),
                     ("l1a", 1, r1_ready, 2, 1), ("l1b", 1, r1_ready, 2, 2), ("ctxT", 3, ctxT_ready, 1, 1),
                     ("max0", 1, max_rows_ready, 2, 1), ("o", 3, out_ready, 1, 1), ("v", 1, v_ready, 1, 1),
                     ("l2", 1, y_ready, 1, 1)]

            def take_bank(s, name):
                users = [u for u in USERS if BANK[u[0]] == BANK[name]]
                at = [u[0] for u in users].index(name)
                for back in range(1, len(users) + 1):
                    _, lag, done, per_batch, k = users[(at - back) % len(users)]
                    lag += 1 if back > at else 0
                    if s.has(lag):
                        s.wait(pe, done, per_batch, lag, k)
                        break
                return psum(name)

            def scores_for_exp(s, t):
                if t % HALF == 0:
                    s.wait(pe, max_rows_loaded[t // HALF], 16, 2, 16)
                s.wait(pe, probs_ready, HEADS, 2, t - 1)
                q, k = q_rows[s.par(2)], k_rows[s.par(2)]
                for kt in range(TT):
                    c = t * SEQ + kt * P
                    last = mm(st_bank[t % 2][:, kt * SEQ:(kt + 1) * SEQ], k[0:MROWS, c:c + P],
                              q[0:MROWS, t * SEQ:(t + 1) * SEQ], start=True, stop=True)
                last.then_inc(st_psum, 1)

            def scores_for_max(s, t):
                if t % HALF == 0:
                    s.wait(pe, rows_loaded[t // HALF], LOADS, 1, LOADS)
                s.wait(pe, max_ready, HEADS, 1, t - 1)
                q, k = q_rows[s.par(1)], k_rows[s.par(1)]
                for qt in range(TT):
                    c = t * SEQ + qt * P
                    last = mm(s_bank[t % 2][:, qt * SEQ:(qt + 1) * SEQ], q[0:ROWS, c:c + P],
                              k[0:ROWS, t * SEQ:(t + 1) * SEQ], start=True, stop=True)
                last.then_inc(s_psum, 1)

            def context(s, lag, g):
                s.wait(pe, probs_ready, HEADS, lag, GROUP * (g + 1))
                s.wait(pe, ctx_copied, GROUPS, lag, g)
                if g == 0:
                    s.wait(pe, v_ready, 1, lag, 1)
                for kt in range(TT):
                    for j in range(GROUP):
                        last = mm(ctx_bank[VC * j:VC * (j + 1), 0:SEQ], v_ext[s.par(lag)][:, kt, GROUP * g + j, :],
                                  probs[g % 2][:, j, kt, :], start=kt == 0, stop=kt == TT - 1)
                last.then_inc(ctx_psum, 1)

            def max_to_rows(s, lag, half):
                s.wait(pe, max_parts_ready, 2, lag, half + 1)
                b = take_bank(s, f"max{half}")[:, :].bitcast(bf16)
                nc.tensor.transpose(b[:, 0:P], max_part[:, half, :], ident16[:, :]).then_inc(maxT_psum, 1)

            def layer0(s, k, b):
                for m in range(2):
                    c = (2 * k + m) * P
                    for n, part in enumerate((xT_hi, xT_lo)):
                        last = mm(b[:, m * SEQ:(m + 1) * SEQ], w0[:, c:c + P], part[s.par(1)][:, :],
                                  start=n == 0, stop=n == 1)
                last.then_inc(l0_psum, 1)

            def layer1_block(b, m):
                for kk in range(FB):
                    for n, part in enumerate((r0_hi, r0_lo)):
                        last = mm(b[:, (m % 2) * SEQ:(m % 2 + 1) * SEQ], w1[:, kk, m * P:(m + 1) * P],
                                  part[:, kk, :], start=kk == n == 0, stop=kk == FB - 1 and n == 1)
                return last

            def layer2_tile(b, t):
                for kk in range(FB):
                    for n, part in enumerate((r1_hi, r1_lo)):
                        last = mm(b[:, t * HID:(t + 1) * HID], part[:, kk, t * P:(t + 1) * P], w2[:, kk, :],
                                  start=kk == n == 0, stop=kk == FB - 1 and n == 1)
                return last

            def turn_context(s, q):
                b = take_bank(s, f"turn{q}")
                for g in range(GROUPS):
                    last = nc.tensor.transpose(b[:, g * P:(g + 1) * P], ctx_sb[:, g, q * P:(q + 1) * P], ident[:, :])
                last.then_inc(ctx_turned, 1)

            def step(s):
                for t in range(HEADS):
                    if s.has(2):
                        scores_for_exp(s, t)
                    if s.has(1):
                        scores_for_max(s, t)
                    if t == 0 and s.has(1):
                        if s.first == 1:
                            pe.wait_ge(ffn_weights_ready, 1)
                        s.wait(pe, xT_split, 1, 1, 1)
                        layer0(s, 0, take_bank(s, "l0a"))
                    if t == 0 and s.has(0):
                        s.wait(pe, xn_ready, 1, 0, 1)
                        b = take_bank(s, "xT")
                        for tt in range(TT):
                            last = nc.tensor.transpose(b[:, tt * P:(tt + 1) * P], xn[:, tt, :], ident[:, :])
                        last.then_inc(xT_psum, 1)
                    if t == 1 and s.has(3):
                        context(s, 3, GROUPS - 1)
                    if t == 2 and s.has(1):
                        layer0(s, 1, take_bank(s, "l0b"))
                    if t == 3 and s.has(2):
                        max_to_rows(s, 2, 1)
                    if t == 4 and s.has(0):
                        s.wait(pe, xT_copied, 2, 0, 1)
                        b = take_bank(s, "qk")
                        for n in range(2):
                            last = mm(b[:, n * SEQ:(n + 1) * SEQ], w_sb[:, n, :], xT[s.par(0)][:, :],
                                      start=True, stop=True)
                        last.then_inc(qk_psum, 1)
                    if t == 4 and s.has(3):
                        s.wait(pe, ctx_copied, GROUPS, 3, GROUPS)
                        turn_context(s, 0)
                    if t == 5 and s.has(2):
                        context(s, 2, 0)
                    if t == 6 and s.has(3):
                        turn_context(s, 1)
                    if t == 6 and s.has(1):
                        s.wait(pe, r0_ready, 2, 1, 2)
                        layer1_block(take_bank(s, "l1a"), 0)
                    if t == 7 and s.has(1):
                        layer1_block(psum("l1a"), 1).then_inc(l1_psum, 1)
                    if t == 8 and s.has(1):
                        layer1_block(take_bank(s, "l1b"), 2)
                    if t == 8 and s.has(3):
                        s.wait(pe, ctxn_ready, TT, 3, TT)
                        b = take_bank(s, "ctxT")
                        for q in range(TT):
                            last = nc.tensor.transpose(b[:, q * P:(q + 1) * P], ctxn[:, q, :], ident[:, :])
                        last.then_inc(ctxT_psum, 1)
                    if t == 9 and s.has(2):
                        context(s, 2, 1)
                    if t == 10 and s.has(1):
                        layer1_block(psum("l1b"), 3).then_inc(l1_psum, 1)
                        max_to_rows(s, 1, 0)
                    if t == 11 and s.has(3):
                        s.wait(pe, ctxT_ready, 1, 3, 1)
                        b = take_bank(s, "o")
                        for q in range(TT):
                            last = mm(b[:, q * HID:(q + 1) * HID], ctxT[:, q * P:(q + 1) * P], w_sb[:, 3, :],
                                      start=True, stop=True)
                        last.then_inc(o_psum, 1)
                    if t == 13 and s.has(1):
                        b = take_bank(s, "v")
                        for kt in range(TT):
                            last = mm(b[:, kt * HID:(kt + 1) * HID], xT[s.par(1)][:, kt * P:(kt + 1) * P],
                                      w_sb[:, 2, :], start=True, stop=True)
                        last.then_inc(v_psum, 1)
                    if t == 13 and s.has(2):
                        context(s, 2, 2)
                    if t == 14 and s.has(1):
                        s.wait(pe, r1_ready, 2, 1, 2)
                        layer2_tile(take_bank(s, "l2"), 0)
                    if t == 15 and s.has(1):
                        layer2_tile(psum("l2"), 1).then_inc(l2_psum, 1)

            pe.wait_ge(ident_ready, 2)
            pe.wait_ge(weights_loaded, 16 * N_WEIGHT_DMAS)
            run_steps(pe, step)


def kernel(L0_attn_x, L0_attn_w_q, L0_attn_s_q, L0_attn_b_q, L0_attn_w_k, L0_attn_s_k, L0_attn_b_k,
           L0_attn_w_v, L0_attn_s_v, L0_attn_b_v, L0_attn_w_o, L0_attn_s_o, L0_attn_b_o,
           L0_ffn_k0, L0_ffn_k1, L0_ffn_k2, L0_ffn_s0, L0_ffn_s1, L0_ffn_s2):
    import numpy as np
    import concourse.bacc as bacc
    from concourse.bass_utils import run_bass_kernel_spmd

    def by_half_dim_head(a):
        a = np.asarray(a)
        return np.swapaxes(a.reshape(a.shape[:-1] + (2, HALF, DH)), -1, -2).reshape(a.shape)

    w4 = np.stack([by_half_dim_head(np.asarray(L0_attn_w_q).T), by_half_dim_head(np.asarray(L0_attn_w_k).T),
                   np.asarray(L0_attn_w_v).T, np.asarray(L0_attn_w_o).T], axis=1)
    arrays = {
        "x": np.asarray(L0_attn_x),
        "w4": w4,
        "bqkv": np.stack([by_half_dim_head(L0_attn_b_q), by_half_dim_head(L0_attn_b_k), np.asarray(L0_attn_b_v)],
                         axis=1),
        "bo": np.asarray(L0_attn_b_o)[None, :],
        "sc7": np.stack([np.asarray(v).reshape(()) for v in (
            L0_attn_s_q, L0_attn_s_k, L0_attn_s_v, L0_attn_s_o, L0_ffn_s0, L0_ffn_s1, L0_ffn_s2)])[None, :],
        "k0": np.ascontiguousarray(L0_ffn_k0).view(np.uint32),
        "k1": np.ascontiguousarray(L0_ffn_k1).view(np.uint32),
        "k2": np.ascontiguousarray(L0_ffn_k2).view(np.uint32),
    }
    arrays = {n: np.ascontiguousarray(a) for n, a in arrays.items()}
    nc = bacc.Bacc("TRN2", target_bir_lowering=False, num_devices=1)
    args = [nc.dram_tensor(n, a.shape, mybir.dt.from_np(a.dtype), kind="ExternalInput").ap()
            for n, a in arrays.items()]
    out = nc.dram_tensor("out", (BATCH, SEQ, HID), mybir.dt.float32, kind="ExternalOutput").ap()
    build(nc, *args, out)
    r = run_bass_kernel_spmd(nc, [arrays], core_ids=[0])
    return r.results[0]["out"]
```

```python
from contextlib import ExitStack

import concourse.bass as bass
from concourse import mybir

BATCH, SEQ, HID = 16, 256, 128
HEADS, DH = 16, 8
HALF = HEADS // 2
FEAT = 512
P = 128
TT = SEQ // P
FB = FEAT // P
PARTS = 3
ROWS = DH * PARTS * PARTS
MROWS = ROWS + PARTS
GROUP = 4
GROUPS = HEADS // GROUP
VC = 32
EPS = 1e-5
EXP_SCALE = float(DH) ** -0.5
X_UP = 2.0 ** 12
W0_DOWN = 2.0 ** -4
W1_DOWN = 2.0 ** -9
FFN_SCALE = 2.0 * 2.0 * 2.0 / (X_UP * W0_DOWN * W1_DOWN)
LOOP_FIRST, LOOP_STEPS = 3, 12
LAST_STEP = BATCH + 2
WARM_START, WARM_FIRST_STEP = 16, 30
L2_LAG = 1
TURN = 32
PE_SLOT = {"xT": 0, "l2_0": 0, "l2_1": 1, "qk": 3, "max1": 3, "ctx3": 4, "l0a": 4, "l0b": 5,
           "ctx0": 6, "l1_0": 8, "l1_1": 9, "ctx1": 9, "max0": 10, "l1_2": 10, "l1_3": 11, "v": 12,
           "ctx2": 14, "o": 14}
ACT_SLOT = {"xT": 1, "ffn": 2, "max1": 3, "qk": 3, "r0a": 4, "r0b": 5, "mid": 7, "ctxT": 8, "r1a": 9,
            "max0": 11, "r1b": 12, "v": 13}
DVE_SLOT = {"split1": 1, "ctx3": 4, "rden": 4, "r0a": 5, "r0b": 6, "back": 7, "ctx0": 7,
            "split0": 7, "stats": 9, "ctx1": 9, "r1a": 10, "meanvar": 11, "r1b": 13, "ctx2": 14, "out": 14}
BANK = {"qk": 0, "l0b": 0, "l1a": 0, "o": 0, "l0a": 1, "l1b": 1, "l2": 1, "xT": 2, "max1": 1, "max0": 2,
        "v": 2}


class Step:

    def __init__(self, first, loop=None):
        self.first, self.loop = first, loop

    def count(self, per_step, const):
        if self.loop is None:
            return per_step * self.first + const
        return self.loop * (2 * per_step) + (per_step * self.first + const)

    def has(self, lag):
        return self.loop is not None or 0 <= self.first - lag < BATCH

    def batch(self, lag):
        return self.count(1, -lag)

    def par(self, lag):
        return (self.first - lag) % 2

    def wait(self, eng, sem, per_batch, lag, k):
        v = self.count(per_batch, k - per_batch * lag)
        if self.loop is not None or v > 0:
            eng.wait_ge(sem, v)

    def wait_dma(self, eng, sems, lag, later=1):
        q = self.par(lag)
        v = self.count(8, -8 * lag - 8 * q + 16 * later)
        if self.loop is not None or v > 0:
            eng.wait_ge(sems[q], v)


def run_steps(eng, step):
    for i in range(-1, LOOP_FIRST):
        step(Step(i))
    with eng.Fori(0, LOOP_STEPS // 2) as it:
        step(Step(LOOP_FIRST, it))
        step(Step(LOOP_FIRST + 1, it))
    for i in range(LOOP_FIRST + LOOP_STEPS, LAST_STEP + 1):
        step(Step(i))


def build(nc, x, w4, bqkv, bo, sc7, k0, k1, k2, out):
    f32, bf16, f16, u8 = mybir.dt.float32, mybir.dt.bfloat16, mybir.dt.float16, mybir.dt.uint8
    ALU, ACT, AX = mybir.AluOpType, mybir.ActivationFunctionType, mybir.AxisListType

    q_scratch = nc.dram_tensor("q_scratch", (2, PARTS * DH, HALF, SEQ), bf16, kind="Internal").ap()
    k_scratch = nc.dram_tensor("k_scratch", (2, DH * PARTS, HALF, SEQ), bf16, kind="Internal").ap()

    with ExitStack() as ctx:
        def sb(name, shape, dt):
            return ctx.enter_context(nc.sbuf_tensor(name, shape, dt))

        def sem(name):
            return ctx.enter_context(nc.semaphore(name))

        w_sb = sb("w_sb", [P, 4, HID], f32)
        bqkv_sb = sb("bqkv_sb", [P, 3], f32)
        bo_sb = sb("bo_sb", [P, 1, HID], f32)
        sc_sb = sb("sc_sb", [P, 7], f32)
        k0_sb = sb("k0_sb", [P, 2, FEAT], u8)
        k1_sb = sb("k1_sb", [P, FB, FEAT], u8)
        k2_sb = sb("k2_sb", [P, FB, HID], u8)
        w0d = sb("w0d", [P, FEAT], f16)
        w0 = sb("w0", [P, FEAT], f16)
        w1 = sb("w1", [P, FB, FEAT], f16)
        w2 = sb("w2", [P, FB, HID], f16)
        sc_down = sb("sc_down", [P, 3], f32)
        sgn = sb("sgn", [P, 8], f32)
        ffn_scale = sb("ffn_scale", [P, 1], f32)
        ident = sb("ident", [P, P], f32)
        ident16 = sb("ident16", [P, P], bf16)
        xin = [sb(f"xin{n}", [P, TT, HID], f32) for n in range(2)]
        stats = sb("stats", [P, TT, 6], f32)
        meanvar = sb("meanvar", [P, TT, 2], f32)
        var_eps = sb("var_eps", [P, TT], f32)
        eps = sb("eps", [P, TT], f32)
        table_load = sb("table_load", [P, TT], f32)
        minus_half = sb("minus_half", [P, TT], f32)
        rstd = sb("rstd", [P, TT], f32)
        xn = sb("xn", [P, TT, HID], f32)
        xres = [sb(f"xres{n}", [P, TT, HID], f32) for n in range(2)]
        xT = [sb(f"xT{n}", [P, SEQ], f32) for n in range(2)]
        xT_hi = [sb(f"xT_hi{n}", [P, SEQ], f16) for n in range(2)]
        xT_lo = [sb(f"xT_lo{n}", [P, SEQ], f16) for n in range(2)]
        qk = sb("qk", [P, 2, SEQ], f32)
        qk_rest = sb("qk_rest", [P, 2, SEQ], f32)
        qk_part = sb("qk_part", [P, PARTS, 2, SEQ], bf16)
        q_rows = [sb(f"q_rows{n}", [P, HEADS * SEQ], bf16) for n in range(2)]
        k_rows = [sb(f"k_rows{n}", [P, HEADS * SEQ], bf16) for n in range(2)]
        neg_max = sb("neg_max", [P, 2, HALF, TT], f32)
        max_rest = sb("max_rest", [P, 2, HALF * TT], f32)
        max_part = sb("max_part", [P, 2, P], bf16)
        max_rows = [sb(f"max_rows{n}", [PARTS * HALF * TT, P], bf16) for n in range(2)]
        v_ext = [sb(f"v_ext{n}", [P, TT, HEADS, VC], f32) for n in range(2)]
        r0_hi = sb("r0_hi", [P, FB, SEQ], f16)
        r0_lo = sb("r0_lo", [P, FB, SEQ], f16)
        r1_hi = sb("r1_hi", [P, FB, SEQ], f16)
        r1_lo = sb("r1_lo", [P, FB, SEQ], f16)
        ffn = [sb(f"ffn{n}", [P, TT, HID], f32) for n in range(2)]
        y = [sb(f"y{n}", [P, TT, HID], f32) for n in range(2)]
        ones = sb("ones", [PARTS, SEQ], bf16)
        probs = [sb(f"probs{n}", [P, GROUP, TT, SEQ], f32) for n in range(2)]
        turned = sb("turned", [P, GROUPS, SEQ // TURN, VC], f32)
        rden = sb("rden", [P, GROUPS, SEQ // TURN], f32)
        ctxn = sb("ctxn", [P, SEQ // TURN, GROUPS, DH], f32)
        ctx_back = sb("ctx_back", [P, SEQ], f32)
        ctxT = sb("ctxT", [P, SEQ], f32)
        outs = [sb(f"outs{n}", [P, TT, HID], f32) for n in range(2)]

        def bank(name):
            return ctx.enter_context(nc.psum_tensor(name, [P, 2 * SEQ], f32))

        s_bank = [bank(f"s_bank{n}") for n in range(2)]
        st_bank = [bank(f"st_bank{n}") for n in range(2)]
        ctx_bank = bank("ctx_bank")
        work = [bank(f"work{n}") for n in range(3)]
        def max_banks(s):
            return s_bank if s.has(2) else s_bank + st_bank

        def exp_banks(s):
            return st_bank if s.has(1) else st_bank + s_bank

        def psum(name):
            return work[BANK[name]]


        attn_weights_loaded = sem("attn_weights_loaded")
        bo_loaded = sem("bo_loaded")
        ffn_weights_loaded = sem("ffn_weights_loaded")
        x_loaded = [sem(f"x_loaded{n}") for n in range(2)]
        k_stored = sem("k_stored")
        q_stored = [sem(f"q_stored{h}") for h in range(2)]
        rows_loaded = [sem(f"rows_loaded{n}") for n in range(2)]
        max_rows_loaded = [sem(f"max_rows_loaded{n}") for n in range(2)]
        out_stored = [sem(f"out_stored{n}") for n in range(2)]
        ident_zeroed = sem("ident_zeroed")
        ident_ready = sem("ident_ready")
        ones_ready = sem("ones_ready")
        ones_loaded = sem("ones_loaded")
        v_zeroed = sem("v_zeroed")
        v_ones_ready = sem("v_ones_ready")
        setup_step = sem("setup_step")
        sc_down_ready = sem("sc_down_ready")
        w0_ready = sem("w0_ready")
        w12_ready = sem("w12_ready")
        ln_step = sem("ln_step")
        half_ready = sem("half_ready")
        meanvar_ready = sem("meanvar_ready")
        ln_pool_step = sem("ln_pool_step")
        xn_centred = sem("xn_centred")
        xn_ready = sem("xn_ready")
        xres_ready = sem("xres_ready")
        xT_psum = sem("xT_psum")
        xT_copied = sem("xT_copied")
        xT_split = sem("xT_split")
        qk_psum = sem("qk_psum")
        qk_scaled = sem("qk_scaled")
        qk_hi_ready = sem("qk_hi_ready")
        qk_rest_ready = sem("qk_rest_ready")
        qk_mid_ready = sem("qk_mid_ready")
        parts_ready = sem("parts_ready")
        s_psum = sem("s_psum")
        max_ready = sem("max_ready")
        max_split_step = sem("max_split_step")
        max_part_zeroed = sem("max_part_zeroed")
        max_parts_ready = sem("max_parts_ready")
        maxT_psum = sem("maxT_psum")
        max_rows_ready = sem("max_rows_ready")
        v_psum = sem("v_psum")
        v_ready = sem("v_ready")
        l0_psum = sem("l0_psum")
        r0_hi_ready = sem("r0_hi_ready")
        r0_ready = sem("r0_ready")
        l1_psum = sem("l1_psum")
        r1_hi_ready = sem("r1_hi_ready")
        r1_ready = sem("r1_ready")
        l2_psum = sem("l2_psum")
        ffn_ready = sem("ffn_ready")
        y_ready = sem("y_ready")
        st_psum = sem("st_psum")
        probs_ready = sem("probs_ready")
        ctx_psum = sem("ctx_psum")
        ctx_turned = sem("ctx_turned")
        rden_ready = sem("rden_ready")
        ctxn_ready = sem("ctxn_ready")
        ctx_back_ready = sem("ctx_back_ready")
        ctxT_ready = sem("ctxT_ready")
        o_psum = sem("o_psum")
        out_ready = sem("out_ready")

        N_ATTN_DMAS = 3
        N_FFN_DMAS = 3
        LOADS = 16 * 2
        block = ctx.enter_context(nc.Block())

        def split_xT(s, engine, eng):
            s.wait(eng, xT_copied, 2, 0, 2)
            s.wait(eng, l0_psum, 2, 2, 2)
            engine.tensor_tensor(xT_lo[s.par(0)][:, :], xT[s.par(0)][:, :], xT_hi[s.par(0)][:, :],
                                 ALU.subtract).then_inc(xT_split, 1)

        def split_qk(s, engine, eng, link):
            if link == 0:
                s.wait(eng, qk_hi_ready, 1, 0, 1)
                engine.tensor_tensor(qk_rest[:, :, :], qk[:, :, :], qk_part[:, 0], ALU.subtract
                                     ).then_inc(qk_rest_ready, 1)
            else:
                s.wait(eng, qk_mid_ready, 1, 0, 1)
                engine.tensor_tensor(qk_part[:, 2], qk_rest[:, :, :], qk_part[:, 1], ALU.subtract
                                     ).then_inc(parts_ready, 1)

        @block.sync
        def _(sp):
            def step(s):
                load_batch = sp.snap(s.batch(-1)) if s.loop is not None else s.batch(-1)
                store_batch = sp.snap(s.batch(3)) if s.loop is not None else s.batch(3)
                rows_free = [s.count(HEADS, HALF * (h + 1) - 2 * HEADS) for h in range(2)]
                rows_read = s.count(LOADS, 0)
                if s.loop is not None:
                    rows_read = sp.snap(sp.to_reg(rows_read))
                    rows_free = [sp.snap(sp.to_reg(v)) for v in rows_free]
                if s.has(2):
                    s.wait(sp, max_rows_ready, 2, 2, 2)
                    sp.dma_start(q_rows[s.par(2)][ROWS:MROWS, HALF * SEQ:], max_rows[1][:, :]
                                 ).then_inc(max_rows_loaded[1], 16)
                if s.has(-1):
                    s.wait(sp, xn_ready, 1, 1, 1)
                    s.wait(sp, xres_ready, 1, 1, 1)
                    sp.dma_start(xin[s.par(-1)][:, :, :],
                                 x[bass.ds(load_batch, 1), :, :].rearrange("a (t p) c -> p (a t) c", p=P)
                                 ).then_inc(x_loaded[s.par(-1)], 16)
                if s.first == -1:
                    load_weights()
                if s.has(0):
                    k_dst = k_scratch.rearrange("h (d r) e t -> r (h d) e t", r=PARTS)
                    for r, ready in enumerate((qk_hi_ready, qk_mid_ready, parts_ready)):
                        s.wait(sp, ready, 1, 0, 1)
                        if r == 0 and s.has(1):
                            for h in range(2):
                                sp.wait_ge(rows_loaded[h], rows_read)
                        sp.dma_start(k_dst[r], qk_part[:, r, 1, :]).then_inc(k_stored, 16)
                    for h in range(2):
                        sp.dma_start(q_scratch[h].rearrange("(r d) e t -> (d e) r t", r=PARTS),
                                     qk_part[h * P // 2:(h + 1) * P // 2, :, 0, :]).then_inc(q_stored[h], 16)
                for h in range(2):
                    if h == 1 and s.has(1):
                        s.wait(sp, max_rows_ready, 2, 1, 1)
                        sp.dma_start(q_rows[s.par(1)][ROWS:MROWS, :HALF * SEQ], max_rows[0][:, :]
                                     ).then_inc(max_rows_loaded[0], 16)
                    if h == 1 and s.has(3):
                        s.wait(sp, out_ready, 1, 3, 1)
                        sp.dma_start(out[bass.ds(store_batch, 1), :, :].rearrange("a (t p) c -> p (a t) c", p=P),
                                     outs[s.par(3)][:, :, :]).then_inc(out_stored[s.par(3)], 16)
                    if s.has(0):
                        cols = slice(h * HALF * SEQ, (h + 1) * HALF * SEQ)
                        if h == 0:
                            s.wait(sp, k_stored, 16 * PARTS, 0, 16 * PARTS)
                        if s.has(2):
                            sp.wait_ge(st_psum, rows_free[h])
                        k_src = k_scratch[h:h + 1].rearrange("x r e t -> x r (e t)")
                        sp.dma_start(k_rows[s.par(0)][0:ROWS, cols],
                                     k_src.to_broadcast([PARTS, DH * PARTS, HALF * SEQ])
                                     ).then_inc(rows_loaded[h], 16)
                        s.wait(sp, q_stored[h], 16, 0, 16)
                        q_src = q_scratch[h].rearrange("(r x) e t -> r x (e t)", x=1)
                        sp.dma_start(q_rows[s.par(0)][0:ROWS, cols],
                                     q_src.to_broadcast([PARTS * DH, PARTS, HALF * SEQ])
                                     ).then_inc(rows_loaded[h], 16)
                if s.first == 0:
                    sp.wait_ge(ones_ready, 1)
                    for n in range(2):
                        sp.dma_start(k_rows[n][ROWS:MROWS, :],
                                     ones[:, :].rearrange("r (x t) -> r x t", x=1).to_broadcast([PARTS, HEADS, SEQ])
                                     ).then_inc(ones_loaded, 16)

            def load_weights():
                u32 = mybir.dt.uint32
                for dst, src, loaded in (
                        (w_sb[:, :, :], w4, attn_weights_loaded),
                        (sc_sb[:, :], sc7.to_broadcast([P, 7]), attn_weights_loaded),
                        (bqkv_sb[:, :], bqkv, attn_weights_loaded),
                        (k0_sb[:, :, :].bitcast(u32), k0.rearrange("(a p) f -> p a f", p=P), ffn_weights_loaded),
                        (k1_sb[:, :, :].bitcast(u32), k1.rearrange("(a p) f -> p a f", p=P), ffn_weights_loaded),
                        (k2_sb[:, :, :].bitcast(u32), k2.rearrange("(a p) f -> p a f", p=P), ffn_weights_loaded),
                        (bo_sb[:, 0, :], bo.to_broadcast([P, HID]), bo_loaded)):
                    sp.dma_start(dst, src).then_inc(loaded, 16)

            run_steps(sp, step)
            for n in range(2):
                sp.wait_ge(out_stored[n], 16 * BATCH // 2)

        @block.gpsimd
        def _(pool):
            def step(s):
                if s.has(2):
                    s.wait(pool, ffn_ready, 1, 2, 1)
                    s.wait(pool, xres_ready, 1, 2, 1)
                    s.wait(pool, out_ready, 1, 4, 1)
                    nc.gpsimd.tensor_tensor(y[s.par(2)][:, :, :], ffn[s.par(2)][:, :, :], xres[s.par(2)][:, :, :],
                                            ALU.add).then_inc(y_ready, 1)
                if s.has(0):
                    residual(s)
                    if s.first != 0:
                        split_xT(s, nc.gpsimd, pool)
                if s.has(3):
                    s.wait(pool, rden_ready, 1, 3, 1)
                    s.wait(pool, ctx_turned, GROUPS, 3, GROUPS)
                    s.wait(pool, ctx_back_ready, 1, 4, 1)
                    nc.gpsimd.tensor_tensor(
                        ctxn[:, :, :, :].rearrange("p b g d -> p g b d"), turned[:, :, :, 0:DH],
                        rden[:, :, :].unsqueeze(3).to_broadcast([P, GROUPS, SEQ // TURN, DH]), ALU.mult
                        ).then_inc(ctxn_ready, 1)
                if s.has(0) and s.first != 0:
                    split_qk(s, nc.gpsimd, pool, 0)
                    split_qk(s, nc.gpsimd, pool, 1)
                if s.first == 0:
                    for n in range(2):
                        nc.gpsimd.memset(v_ext[n][:, :, :, :], 0.0).then_inc(v_zeroed, 1)
                    pool.wait_ge(v_zeroed, 2)
                    for n in range(2):
                        nc.gpsimd.memset(v_ext[n][:, :, :, DH:DH + 1], 1.0).then_inc(v_ones_ready, 1)
                if s.has(-1):
                    s.wait(pool, meanvar_ready, TT, -1, TT)
                    nc.gpsimd.tensor_tensor(var_eps[:, :], meanvar[:, :, 1], eps[:, :], ALU.add
                                            ).then_inc(ln_pool_step, 1)
                    if s.first >= 0:
                        s.wait(pool, xT_psum, 1, 0, 1)
                        nc.gpsimd.tensor_tensor(xn[:, :, :], xin[s.par(-1)][:, :, :],
                                                meanvar[:, :, 0:1].to_broadcast([P, TT, HID]), ALU.subtract
                                                ).then_inc(xn_centred, 1)
                    s.wait(pool, ln_pool_step, 2, -1, 1)
                    nc.gpsimd.tensor_tensor(rstd[:, :], var_eps[:, :], minus_half[:, :], ALU.pow
                                            ).then_inc(ln_pool_step, 1)
                    if s.first >= 0:
                        s.wait(pool, ln_pool_step, 2, -1, 2)
                        s.wait(pool, xn_centred, 1, 0, 1)
                        nc.gpsimd.tensor_tensor(xn[:, :, :], xn[:, :, :],
                                                rstd[:, :].unsqueeze(2).to_broadcast([P, TT, HID]), ALU.mult
                                                ).then_inc(xn_ready, 1)

            def residual(s):
                if s.first == 0:
                    pool.wait_ge(bo_loaded, 16)
                s.wait_dma(pool, x_loaded, 0)
                s.wait(pool, y_ready, 1, 2, 1)
                nc.gpsimd.tensor_tensor(xres[s.par(0)][:, :, :], xin[s.par(0)][:, :, :],
                                        bo_sb[:, :, :].to_broadcast([P, TT, HID]), ALU.add
                                        ).then_inc(xres_ready, 1)

            nc.gpsimd.memset(minus_half[:, :], -0.5).then_inc(half_ready, 1)
            nc.gpsimd.memset(eps[:, :], EPS).then_inc(half_ready, 1)
            pool.wait_ge(half_ready, 2)
            nc.gpsimd.memset(ident[:, :], 0.0).then_inc(ident_zeroed, 1)
            nc.gpsimd.memset(ident16[:, :], 0.0).then_inc(ident_zeroed, 1)
            pool.wait_ge(ident_zeroed, 2)
            for m in (ident, ident16):
                nc.gpsimd.affine_select(out=m[:, :], in_=m[:, :], compare_op=ALU.not_equal, fill=1.0, base=0,
                                        pattern=[[-1, P]], channel_multiplier=1).then_inc(ident_ready, 1)
            nc.gpsimd.memset(ones[:, :], 1.0).then_inc(ones_ready, 1)
            run_steps(pool, step)

        @block.scalar
        def _(act):
            def relu_hi(k, b, dst, ready):
                nc.scalar.activation(dst[:, 2 * k:2 * k + 2, :].rearrange("p m t -> p (m t)"), b[:, :],
                                     ACT.Relu).then_inc(ready, 1)

            def step(s):
                for t in range(HEADS):
                    if s.has(2):
                        s.wait(act, st_psum, HEADS, 2, t + 1)
                        if t % GROUP == 0:
                            s.wait(act, ctx_psum, GROUPS, 2, t // GROUP - 1)
                        nc.scalar.activation(
                            probs[t // GROUP % 2][:, t % GROUP, :, :].rearrange("p k q -> p (k q)"),
                            exp_banks(s)[t % len(exp_banks(s))][:, :], ACT.Exp, scale=EXP_SCALE).then_inc(probs_ready, 1)
                    if t == ACT_SLOT["ffn"] and s.has(1):
                        if s.first == 1:
                            act.wait_ge(w12_ready, 3)
                        s.wait(act, l2_psum, 1, 1, 1)
                        s.wait(act, y_ready, 1, 3, 1)
                        nc.scalar.activation(ffn[s.par(1)][:, :, :].rearrange("p t c -> p (t c)"),
                                             psum("l2")[:, 0:TT * HID], ACT.Copy, scale=ffn_scale[:, :]
                                             ).then_inc(ffn_ready, 1)
                    for half in range(2):
                        lag = 1 + half
                        if t == ACT_SLOT[f"max{half}"] and s.has(lag):
                            s.wait(act, maxT_psum, 2, lag, half + 1)
                            s.wait(act, max_rows_loaded[half], 16, lag + 1, 16)
                            src = psum(f"max{half}")[:, :].bitcast(bf16)
                            nc.scalar.activation(max_rows[half][:, :], src[0:PARTS * HALF * TT, 0:P], ACT.Copy
                                                 ).then_inc(max_rows_ready, 1)
                    if t == ACT_SLOT["xT"] and s.has(0):
                        s.wait(act, xT_psum, 1, 0, 1)
                        s.wait(act, v_psum, 1, 2, 1)
                        s.wait(act, l0_psum, 2, 2, 2)
                        b = psum("xT")[:, 0:SEQ]
                        nc.scalar.activation(xT[s.par(0)][:, :], b, ACT.Copy, scale=X_UP).then_inc(xT_copied, 1)
                        nc.scalar.activation(xT_hi[s.par(0)][:, :], b, ACT.Copy, scale=X_UP).then_inc(xT_copied, 1)
                    if t == ACT_SLOT["qk"] and s.has(0):
                        if s.first == 0:
                            act.wait_ge(sc_down_ready, 1)
                        s.wait(act, qk_psum, 1, 0, 1)
                        s.wait(act, parts_ready, 1, 1, 1)
                        s.wait(act, k_stored, 16 * PARTS, 1, 16 * PARTS)
                        for h in range(2):
                            s.wait(act, q_stored[h], 16, 1, 16)
                        for n in range(2):
                            nc.scalar.activation(qk[:, n, :], psum("qk")[:, n * SEQ:(n + 1) * SEQ], ACT.Identity,
                                                 scale=sc_down[:, n:n + 1], bias=bqkv_sb[:, n:n + 1]
                                                 ).then_inc(qk_scaled, 1)
                        s.wait(act, qk_scaled, 2, 0, 2)
                        nc.scalar.activation(qk_part[:, 0], qk[:, :, :], ACT.Copy).then_inc(qk_hi_ready, 1)
                    if t == ACT_SLOT["r0a"] and s.has(0):
                        s.wait(act, l0_psum, 2, 0, 1)
                        s.wait(act, l1_psum, 2, 1, 2)
                        relu_hi(0, psum("l0a"), r0_hi, r0_hi_ready)
                    if t == ACT_SLOT["r0b"] and s.has(0):
                        s.wait(act, l0_psum, 2, 0, 2)
                        relu_hi(1, psum("l0b"), r0_hi, r0_hi_ready)
                    if t == ACT_SLOT["mid"] and s.has(0):
                        s.wait(act, qk_rest_ready, 1, 0, 1)
                        nc.scalar.activation(qk_part[:, 1], qk_rest[:, :, :], ACT.Copy).then_inc(qk_mid_ready, 1)
                    if t == ACT_SLOT["r1a"] and s.has(0):
                        s.wait(act, l1_psum, 2, 0, 1)
                        s.wait(act, l2_psum, 1, 1, 1)
                        relu_hi(0, psum("l1a"), r1_hi, r1_hi_ready)
                    if t == ACT_SLOT["ctxT"] and s.has(3):
                        s.wait(act, ctx_back_ready, 1, 3, 1)
                        s.wait(act, o_psum, 1, 4, 1)
                        nc.scalar.activation(ctxT[:, :], ctx_back[:, :], ACT.Identity, scale=sc_down[:, 2:3],
                                             bias=bqkv_sb[:, 2:3]).then_inc(ctxT_ready, 1)
                    if t == ACT_SLOT["r1b"] and s.has(0):
                        s.wait(act, l1_psum, 2, 0, 2)
                        relu_hi(1, psum("l1b"), r1_hi, r1_hi_ready)
                    if t == ACT_SLOT["v"] and s.has(1):
                        s.wait(act, v_psum, 1, 1, 1)
                        s.wait(act, ctx_psum, GROUPS, 3, GROUPS)
                        if s.first == 1:
                            act.wait_ge(v_ones_ready, 2)
                        nc.scalar.activation(
                            v_ext[s.par(1)][:, :, :, 0:DH],
                            psum("v")[:, 0:TT * HID].rearrange("p (t h d) -> p t h d", t=TT, d=DH), ACT.Copy
                        ).then_inc(v_ready, 1)

            act.wait_ge(half_ready, 2)
            nc.scalar.activation(table_load[:, :], eps[:, :], ACT.Exp)
            act.wait_ge(attn_weights_loaded, 16 * N_ATTN_DMAS)
            run_steps(act, step)

        @block.vector
        def _(dve):
            def token_stats(s):
                s.wait_dma(dve, x_loaded, -1)
                for t in range(TT):
                    nc.vector.bn_stats(stats[:, t, :], xin[s.par(-1)][:, t, :]).then_inc(ln_step, 1)

            def split_max(s, lag, half, link):
                full = neg_max[:, half, :, :].rearrange("p h t -> p (h t)")
                rest = max_rest[:, half, :]
                part = max_part[:, half, 0:PARTS * HALF * TT].rearrange("p (r c) -> p r c", r=PARTS)
                if link == 0:
                    s.wait(dve, max_ready, HEADS, lag, HALF * (half + 1))
                    s.wait(dve, maxT_psum, 2, lag + 1, half + 1)
                    nc.vector.tensor_copy(part[:, 0, :], full).then_inc(max_split_step, 1)
                elif link == 1:
                    s.wait(dve, max_split_step, 6, lag, 3 * half + 1)
                    nc.vector.tensor_tensor(rest, full, part[:, 0, :], ALU.subtract).then_inc(max_split_step, 1)
                elif link == 2:
                    s.wait(dve, max_split_step, 6, lag, 3 * half + 2)
                    nc.vector.tensor_copy(part[:, 1, :], rest).then_inc(max_split_step, 1)
                else:
                    s.wait(dve, max_split_step, 6, lag, 3 * half + 3)
                    nc.vector.tensor_tensor(part[:, 2, :], rest, part[:, 1, :], ALU.subtract
                                            ).then_inc(max_parts_ready, 1)

            def relu_lo(k, b, hi, lo, ready):
                nc.vector.scalar_tensor_tensor(
                    out=lo[:, 2 * k:2 * k + 2, :].rearrange("p m t -> p (m t)"), in0=b[:, :], scalar=0.0,
                    in1=hi[:, 2 * k:2 * k + 2, :].rearrange("p m t -> p (m t)"),
                    op0=ALU.max, op1=ALU.subtract).then_inc(ready, 1)

            def step(s):
                if s.first == -1:
                    token_stats(s)
                    dve.wait_ge(ln_step, TT)
                    for tt in range(TT):
                        nc.vector.bn_aggr(meanvar[:, tt, :], stats[:, tt, :]).then_inc(meanvar_ready, 1)
                    s.wait(dve, ln_pool_step, 2, -1, 2)
                    s.wait(dve, meanvar_ready, TT, -1, TT)
                    for tt in range(TT):
                        last = nc.vector.tensor_scalar(xn[:, tt, :], xin[0][:, tt, :], meanvar[:, tt, 0:1],
                                                       rstd[:, tt:tt + 1], ALU.subtract, ALU.mult)
                    last.then_inc(xn_ready, 1)
                    return
                if s.first == 0:
                    first_layer_weights()
                meanvar_slot = DVE_SLOT["stats"] + 1 if s.first == 0 else DVE_SLOT["meanvar"]
                for t in range(HEADS):
                    if t == meanvar_slot and s.has(-1):
                        s.wait(dve, xn_ready, 1, 0, 1)
                        s.wait(dve, ln_step, TT, -1, TT)
                    if s.has(1):
                        s.wait(dve, s_psum, HEADS, 1, t + 1)
                        nc.vector.tensor_reduce(out=neg_max[:, t // HALF, t % HALF, :],
                                                in_=max_banks(s)[t % len(max_banks(s))][:, :].rearrange("p (q k) -> p q k", q=TT),
                                                op=ALU.max, axis=AX.X, negate=True).then_inc(max_ready, 1)
                    if t == DVE_SLOT["ctx3"] and s.has(3):
                        turn_context(s, 3, GROUPS - 1)
                    for g in range(GROUPS - 1):
                        if t == DVE_SLOT[f"ctx{g}"] and s.has(2):
                            turn_context(s, 2, g)
                    for link in (0, 2):
                        if t == DVE_SLOT["split1"] + link // 2 and s.has(2):
                            split_max(s, 2, 1, link)
                    if t == 2 and s.first == 0:
                        split_xT(s, nc.vector, dve)
                    for link in (1, 3):
                        if t == DVE_SLOT["split1"] + link // 2 and s.has(2):
                            split_max(s, 2, 1, link)
                    if t == 2 and s.first == 0:
                        second_layer_weights(0)
                        split_qk(s, nc.vector, dve, 0)
                        second_layer_weights(1)
                        split_qk(s, nc.vector, dve, 1)
                    if t == 8 and s.first == 0:
                        third_layer_weights()
                    if t == DVE_SLOT["r0a"] and s.has(0):
                        s.wait(dve, r0_hi_ready, 2, 0, 1)
                        s.wait(dve, l1_psum, 2, 1, 2)
                        relu_lo(0, psum("l0a"), r0_hi, r0_lo, r0_ready)
                    if t == DVE_SLOT["r0b"] and s.has(0):
                        s.wait(dve, r0_hi_ready, 2, 0, 2)
                        relu_lo(1, psum("l0b"), r0_hi, r0_lo, r0_ready)
                    if t == DVE_SLOT["rden"] and s.has(3):
                        s.wait(dve, ctx_turned, GROUPS, 3, GROUPS)
                        s.wait(dve, ctxn_ready, 1, 4, 1)
                        nc.vector.reciprocal(rden[:, :, :], turned[:, :, :, DH]).then_inc(rden_ready, 1)
                    if t == DVE_SLOT["back"] and s.has(3):
                        s.wait(dve, ctxn_ready, 1, 3, 1)
                        s.wait(dve, ctxT_ready, 1, 4, 1)
                        nc.vector.transpose(ctx_back[:, :], ctxn[:, :, :, :].rearrange("p b g d -> p (b g d)")
                                            ).then_inc(ctx_back_ready, 1)
                    if t == DVE_SLOT["split0"] and s.has(1):
                        split_max(s, 1, 0, 0)
                        split_max(s, 1, 0, 1)
                    if t == DVE_SLOT["split0"] + 1 and s.has(1):
                        split_max(s, 1, 0, 2)
                        split_max(s, 1, 0, 3)
                    if t == DVE_SLOT["r1a"] and s.has(0):
                        s.wait(dve, r1_hi_ready, 2, 0, 1)
                        s.wait(dve, l2_psum, 1, 1, 1)
                        relu_lo(0, psum("l1a"), r1_hi, r1_lo, r1_ready)
                    if t == DVE_SLOT["stats"] and s.has(-1):
                        token_stats(s)
                    if t == meanvar_slot and s.has(-1):
                        for tt in range(TT):
                            nc.vector.bn_aggr(meanvar[:, tt, :], stats[:, tt, :]).then_inc(meanvar_ready, 1)
                    if t == DVE_SLOT["r1b"] and s.has(0):
                        s.wait(dve, r1_hi_ready, 2, 0, 2)
                        relu_lo(1, psum("l1b"), r1_hi, r1_lo, r1_ready)
                    if t == DVE_SLOT["out"] and s.has(3):
                        s.wait(dve, o_psum, 1, 3, 1)
                        s.wait(dve, y_ready, 1, 3, 1)
                        s.wait_dma(dve, out_stored, 3, later=0)
                        nc.vector.scalar_tensor_tensor(
                            out=outs[s.par(3)][:, :, :].rearrange("p t c -> p (t c)"), in0=psum("o")[:, 0:TT * HID],
                            scalar=sc_sb[:, 3:4], in1=y[s.par(3)][:, :, :].rearrange("p t c -> p (t c)"),
                            op0=ALU.mult, op1=ALU.add).then_inc(out_ready, 1)

            def turn_context(s, lag, g):
                s.wait(dve, ctx_psum, GROUPS, lag, g + 1)
                s.wait(dve, ctxn_ready, 1, lag + 1, 1)
                nc.vector.transpose(turned[:, g, :, :].rearrange("p b c -> p (b c)"), ctx_bank[:, 0:SEQ]
                                    ).then_inc(ctx_turned, 1)

            def first_layer_weights():
                s01 = sc_sb[:, 4:6]
                dve.wait_ge(attn_weights_loaded, 16 * N_ATTN_DMAS)
                nc.vector.tensor_scalar(sc_down[:, :], sc_sb[:, 0:3], 1.0 / X_UP, None, ALU.mult
                                        ).then_inc(sc_down_ready, 1)
                nc.vector.tensor_scalar(sgn[:, 0:2], s01, 0.0, None, ALU.is_gt)
                nc.vector.tensor_scalar(sgn[:, 2:4], s01, 0.0, None, ALU.is_lt).then_inc(setup_step, 1)
                dve.wait_ge(setup_step, 1)
                nc.vector.tensor_tensor(sgn[:, 0:2], sgn[:, 0:2], sgn[:, 2:4], ALU.subtract).then_inc(setup_step, 1)
                dve.wait_ge(setup_step, 2)
                nc.vector.tensor_scalar(sgn[:, 4:5], sgn[:, 0:1], W0_DOWN, None, ALU.mult)
                nc.vector.tensor_scalar(sgn[:, 5:6], sgn[:, 1:2], 2.0 * W1_DOWN, None, ALU.mult)
                nc.vector.tensor_scalar(sgn[:, 6:7], sgn[:, 1:2], -W1_DOWN, None, ALU.mult)
                nc.vector.tensor_tensor(sgn[:, 2:4], sgn[:, 0:2], s01, ALU.mult).then_inc(setup_step, 1)
                dve.wait_ge(ffn_weights_loaded, 16 * N_FFN_DMAS)
                nc.vector.tensor_tensor(w0d[:, :], k0_sb[:, 0, :], k0_sb[:, 1, :], ALU.subtract
                                        ).then_inc(setup_step, 1)
                dve.wait_ge(setup_step, 4)
                nc.vector.tensor_scalar(w0[:, :], w0d[:, :], sgn[:, 4:5], None, ALU.mult).then_inc(w0_ready, 1)

            def second_layer_weights(half):
                blocks = slice(half * FB // 2, (half + 1) * FB // 2)
                nc.vector.tensor_scalar(w1[:, blocks, :], k1_sb[:, blocks, :], sgn[:, 5:6], sgn[:, 6:7],
                                        ALU.mult, ALU.add).then_inc(w12_ready, 1)

            def third_layer_weights():
                nc.vector.scalar_tensor_tensor(out=ffn_scale[:, :], in0=sgn[:, 2:3], scalar=FFN_SCALE,
                                               in1=sgn[:, 3:4], op0=ALU.mult, op1=ALU.mult).then_inc(setup_step, 1)
                nc.vector.tensor_scalar(w2[:, :, :], k2_sb[:, :, :], 2.0, -1.0, ALU.mult, ALU.add)
                dve.wait_ge(setup_step, 5)
                nc.vector.tensor_tensor(ffn_scale[:, :], ffn_scale[:, :], sc_sb[:, 6:7], ALU.mult
                                        ).then_inc(w12_ready, 1)

            nc.vector.memset(max_part[:, :, :], 0.0).then_inc(max_part_zeroed, 1)
            dve.wait_ge(max_part_zeroed, 1)
            run_steps(dve, step)

        @block.tensor
        def _(pe):
            mm = nc.tensor.matmul

            USERS = [("xT", "xT", 0, xT_copied, 2, 2), ("qk", "qk", 0, qk_scaled, 2, 2),
                     ("max1", "max1", 2, max_rows_ready, 2, 2), ("l0a", "l0a", 0, r0_ready, 2, 1),
                     ("l0b", "l0b", 0, r0_ready, 2, 2), ("l1a", "l1_0", 0, r1_ready, 2, 1),
                     ("l1b", "l1_2", 0, r1_ready, 2, 2),
                     ("max0", "max0", 1, max_rows_ready, 2, 1), ("o", "o", 3, out_ready, 1, 1),
                     ("v", "v", 1, v_ready, 1, 1), ("l2", "l2_0", L2_LAG, ffn_ready, 1, 1)]
            USERS.sort(key=lambda u: PE_SLOT[u[1]])

            def take_bank(s, name):
                users = [u for u in USERS if BANK[u[0]] == BANK[name]]
                at = [u[0] for u in users].index(name)
                for back in range(1, len(users) + 1):
                    _, _, lag, done, per_batch, k = users[(at - back) % len(users)]
                    lag += 1 if back > at else 0
                    if s.has(lag):
                        s.wait(pe, done, per_batch, lag, k)
                        break
                return psum(name)

            def scores_for_exp(s, t):
                if t % HALF == 0:
                    s.wait(pe, max_rows_loaded[t // HALF], 16, 2, 16)
                banks = exp_banks(s)
                s.wait(pe, probs_ready, HEADS, 2, t - 1 if t < 2 else t + 1 - len(banks))
                if s.first == 2 and t < 2:
                    s.wait(pe, max_ready, HEADS, 2, HEADS - 1 + t)
                if not s.has(1) and 2 <= t < 4:
                    s.wait(pe, max_ready, HEADS, 2, HEADS - 3 + t)
                q, k = q_rows[s.par(2)], k_rows[s.par(2)]
                for kt in range(TT):
                    c = t * SEQ + kt * P
                    last = mm(banks[t % len(banks)][:, kt * SEQ:(kt + 1) * SEQ], k[0:MROWS, c:c + P],
                              q[0:MROWS, t * SEQ:(t + 1) * SEQ], start=True, stop=True)
                last.then_inc(st_psum, 1)

            def scores_for_max(s, t):
                if t % HALF == 0:
                    s.wait(pe, rows_loaded[t // HALF], LOADS, 1, LOADS)
                banks = max_banks(s)
                s.wait(pe, max_ready, HEADS, 1, t + 1 - len(banks))
                q, k = q_rows[s.par(1)], k_rows[s.par(1)]
                for qt in range(TT):
                    c = t * SEQ + qt * P
                    last = mm(banks[t % len(banks)][:, qt * SEQ:(qt + 1) * SEQ], q[0:ROWS, c:c + P],
                              k[0:ROWS, t * SEQ:(t + 1) * SEQ], start=True, stop=True)
                last.then_inc(s_psum, 1)

            def context(s, lag, g):
                s.wait(pe, probs_ready, HEADS, lag, GROUP * (g + 1))
                s.wait(pe, ctx_turned, GROUPS, lag, g)
                if g == 0:
                    s.wait(pe, v_ready, 1, lag, 1)
                for kt in range(TT):
                    for j in range(GROUP):
                        last = mm(ctx_bank[VC * j:VC * (j + 1), 0:SEQ], v_ext[s.par(lag)][:, kt, GROUP * g + j, :],
                                  probs[g % 2][:, j, kt, :], start=kt == 0, stop=kt == TT - 1)
                last.then_inc(ctx_psum, 1)

            def max_to_rows(s, lag, half):
                s.wait(pe, max_parts_ready, 2, lag, half + 1)
                b = take_bank(s, f"max{half}")[:, :].bitcast(bf16)
                nc.tensor.transpose(b[:, 0:P], max_part[:, half, :], ident16[:, :]).then_inc(maxT_psum, 1)

            def layer0(s, k, b):
                for m in range(2):
                    c = (2 * k + m) * P
                    for n, part in enumerate((xT_hi, xT_lo)):
                        last = mm(b[:, m * SEQ:(m + 1) * SEQ], w0[:, c:c + P], part[s.par(0)][:, :],
                                  start=n == 0, stop=n == 1)
                last.then_inc(l0_psum, 1)

            def layer1_block(b, m):
                for kk in range(FB):
                    for n, part in enumerate((r0_hi, r0_lo)):
                        last = mm(b[:, (m % 2) * SEQ:(m % 2 + 1) * SEQ], w1[:, kk, m * P:(m + 1) * P],
                                  part[:, kk, :], start=kk == n == 0, stop=kk == FB - 1 and n == 1)
                return last

            def layer2_tile(b, t):
                for kk in range(FB):
                    for n, part in enumerate((r1_hi, r1_lo)):
                        last = mm(b[:, t * HID:(t + 1) * HID], part[:, kk, t * P:(t + 1) * P], w2[:, kk, :],
                                  start=kk == n == 0, stop=kk == FB - 1 and n == 1)
                return last

            def keep_warm(n):
                for _ in range(n):
                    nc.tensor.transpose(st_bank[0][:, 0:P], ident[:, :], ident[:, :])

            def step(s):
                for t in range(HEADS):
                    if s.first == 0 and t == PE_SLOT["l1_0"]:
                        keep_warm(WARM_FIRST_STEP)
                    if s.first == 2 and t == 0:
                        pe.wait_ge(ones_loaded, 32)
                    if s.has(2):
                        scores_for_exp(s, t)
                    if s.has(1):
                        scores_for_max(s, t)
                    if t == PE_SLOT["xT"] and s.has(0):
                        s.wait(pe, xn_ready, 1, 0, 1)
                        b = take_bank(s, "xT")
                        for tt in range(TT):
                            last = nc.tensor.transpose(b[:, tt * P:(tt + 1) * P], xn[:, tt, :], ident[:, :])
                        last.then_inc(xT_psum, 1)
                    if t == PE_SLOT["ctx3"] and s.has(3):
                        context(s, 3, GROUPS - 1)
                    if t == PE_SLOT["qk"] and s.has(0):
                        s.wait(pe, xT_copied, 2, 0, 1)
                        b = take_bank(s, "qk")
                        for n in range(2):
                            last = mm(b[:, n * SEQ:(n + 1) * SEQ], w_sb[:, n, :], xT[s.par(0)][:, :],
                                      start=True, stop=True)
                        last.then_inc(qk_psum, 1)
                    if t == PE_SLOT["max1"] and s.has(2):
                        max_to_rows(s, 2, 1)
                    if t == PE_SLOT["l0a"] and s.has(0):
                        if s.first == 0:
                            pe.wait_ge(w0_ready, 1)
                        s.wait(pe, xT_split, 1, 0, 1)
                        layer0(s, 0, take_bank(s, "l0a"))
                    if t == PE_SLOT["l0b"] and s.has(0):
                        layer0(s, 1, take_bank(s, "l0b"))
                    if t == PE_SLOT["ctx0"] and s.has(2):
                        context(s, 2, 0)
                    if t == PE_SLOT["l1_0"] and s.has(0):
                        if s.first == 0:
                            pe.wait_ge(w12_ready, 2)
                        s.wait(pe, r0_ready, 2, 0, 2)
                        layer1_block(take_bank(s, "l1a"), 0)
                    if t == PE_SLOT["l1_1"] and s.has(0):
                        layer1_block(psum("l1a"), 1).then_inc(l1_psum, 1)
                    if t == PE_SLOT["l1_2"] and s.has(0):
                        layer1_block(take_bank(s, "l1b"), 2)
                    if t == PE_SLOT["ctx1"] and s.has(2):
                        context(s, 2, 1)
                    if t == PE_SLOT["l1_3"] and s.has(0):
                        layer1_block(psum("l1b"), 3).then_inc(l1_psum, 1)
                    if t == PE_SLOT["max0"] and s.has(1):
                        max_to_rows(s, 1, 0)
                    if t == PE_SLOT["o"] and s.has(3):
                        s.wait(pe, ctxT_ready, 1, 3, 1)
                        b = take_bank(s, "o")
                        for q in range(TT):
                            last = mm(b[:, q * HID:(q + 1) * HID], ctxT[:, q * P:(q + 1) * P], w_sb[:, 3, :],
                                      start=True, stop=True)
                        last.then_inc(o_psum, 1)
                    if t == PE_SLOT["v"] and s.has(1):
                        b = take_bank(s, "v")
                        for kt in range(TT):
                            last = mm(b[:, kt * HID:(kt + 1) * HID], xT[s.par(1)][:, kt * P:(kt + 1) * P],
                                      w_sb[:, 2, :], start=True, stop=True)
                        last.then_inc(v_psum, 1)
                    if t == PE_SLOT["ctx2"] and s.has(2):
                        context(s, 2, 2)
                    if t == PE_SLOT["l2_0"] and s.has(L2_LAG):
                        if s.first == L2_LAG:
                            pe.wait_ge(w12_ready, 3)
                        s.wait(pe, r1_ready, 2, L2_LAG, 2)
                        layer2_tile(take_bank(s, "l2"), 0)
                    if t == PE_SLOT["l2_1"] and s.has(L2_LAG):
                        layer2_tile(psum("l2"), 1).then_inc(l2_psum, 1)

            pe.wait_ge(ident_ready, 2)
            keep_warm(WARM_START)
            pe.wait_ge(attn_weights_loaded, 16 * N_ATTN_DMAS)
            run_steps(pe, step)


def kernel(L0_attn_x, L0_attn_w_q, L0_attn_s_q, L0_attn_b_q, L0_attn_w_k, L0_attn_s_k, L0_attn_b_k,
           L0_attn_w_v, L0_attn_s_v, L0_attn_b_v, L0_attn_w_o, L0_attn_s_o, L0_attn_b_o,
           L0_ffn_k0, L0_ffn_k1, L0_ffn_k2, L0_ffn_s0, L0_ffn_s1, L0_ffn_s2):
    import numpy as np
    import concourse.bacc as bacc
    from concourse.bass_utils import run_bass_kernel_spmd

    def by_half_dim_head(a):
        a = np.asarray(a)
        return np.swapaxes(a.reshape(a.shape[:-1] + (2, HALF, DH)), -1, -2).reshape(a.shape)

    def by_tile_group(a):
        a = np.asarray(a)
        return np.swapaxes(a.reshape((GROUPS, GROUP, DH) + a.shape[1:]), 0, 1).reshape(a.shape)

    w4 = np.stack([by_half_dim_head(np.asarray(L0_attn_w_q).T), by_half_dim_head(np.asarray(L0_attn_w_k).T),
                   np.asarray(L0_attn_w_v).T, by_tile_group(np.asarray(L0_attn_w_o).T)], axis=1)
    arrays = {
        "x": np.asarray(L0_attn_x),
        "w4": w4,
        "bqkv": np.stack([by_half_dim_head(L0_attn_b_q), by_half_dim_head(L0_attn_b_k), by_tile_group(L0_attn_b_v)],
                         axis=1),
        "bo": np.asarray(L0_attn_b_o)[None, :],
        "sc7": np.stack([np.asarray(v).reshape(()) for v in (
            L0_attn_s_q, L0_attn_s_k, L0_attn_s_v, L0_attn_s_o, L0_ffn_s0, L0_ffn_s1, L0_ffn_s2)])[None, :],
        "k0": np.ascontiguousarray(L0_ffn_k0).view(np.uint32),
        "k1": np.ascontiguousarray(L0_ffn_k1).view(np.uint32),
        "k2": np.ascontiguousarray(L0_ffn_k2).view(np.uint32),
    }
    arrays = {n: np.ascontiguousarray(a) for n, a in arrays.items()}
    nc = bacc.Bacc("TRN2", target_bir_lowering=False, num_devices=1)
    args = [nc.dram_tensor(n, a.shape, mybir.dt.from_np(a.dtype), kind="ExternalInput").ap()
            for n, a in arrays.items()]
    out = nc.dram_tensor("out", (BATCH, SEQ, HID), mybir.dt.float32, kind="ExternalOutput").ap()
    build(nc, *args, out)
    r = run_bass_kernel_spmd(nc, [arrays], core_ids=[0])
    return r.results[0]["out"]
```
